# Optimizing a Trainium2 kernel written in Bass

```python
import numpy as np
import jax
import jax.numpy as jnp

def _softmax(x, axis=-1):
    return jax.nn.softmax(x, axis=axis)

def _gelu(x):
    return jax.nn.gelu(x, approximate=True)

def _silu(x):
    return jax.nn.silu(x)

def _sigmoid(x):
    return jax.nn.sigmoid(x)

def _layernorm(x, axis=-1, eps=1e-05):
    m = jnp.mean(x, axis=axis, keepdims=True)
    v = jnp.var(x, axis=axis, keepdims=True)
    return (x - m) / jnp.sqrt(v + eps)

def _scatter_add(tgt, idx, src, axis=0):
    return tgt.at[idx].add(src)

def _segment_sum(src, seg, n):
    return jax.ops.segment_sum(src, seg, n)
kernel_name = 'mk_gnn_preln_d1_gnn_r64_40eea1'

def setup_inputs(seed: int=0):
    np.random.seed(seed)
    _w = jnp.asarray

    def _rec_inputs():
        import jax
        import jax.numpy as jnp
        _gk = jax.random.key(seed)
        x = -8.776e-05 + 1 * jax.random.normal(jax.random.fold_in(_gk, 1), (100000, 128), jnp.float32)
        src = jax.random.randint(jax.random.fold_in(_gk, 2), (25000,), 0, 100000, jnp.int32)
        dst = jnp.minimum((100000 * jax.random.uniform(jax.random.fold_in(_gk, 3), (25000,)) ** 2.0).astype(jnp.int32), 99999)
        _o = jnp.argsort(dst, stable=True)
        src = src[_o]
        dst = dst[_o]
        edge_attr_64 = 0.000167468 + 1.0002 * jax.random.normal(jax.random.fold_in(_gk, 11), (25000, 64), jnp.float32)
        return (x, src, dst, edge_attr_64)
    x, src, dst, edge_attr_64 = _rec_inputs()

    def _L0_gnn_setup():
        import jax, jax.numpy as jnp
        import numpy as np
        N_NODES = 625
        N_EDGES = 10000
        ATOM_DIM = 128
        BOND_DIM = 64
        HIDDEN = 128
        key = jax.random.key(seed)
        ks = jax.random.split(key, 11)
        x = jax.random.normal(ks[0], (N_NODES, ATOM_DIM), dtype=jnp.float32)
        edge_index = jax.random.randint(ks[1], (2, N_EDGES), 0, N_NODES, dtype=jnp.int64)
        edge_attr = jax.random.normal(ks[2], (N_EDGES, BOND_DIM), dtype=jnp.float32)
        s1 = 1.0 / np.sqrt(ATOM_DIM + BOND_DIM)
        s2 = 1.0 / np.sqrt(HIDDEN)
        s3 = 1.0 / np.sqrt(ATOM_DIM + HIDDEN)
        msg_w1 = jax.random.uniform(ks[3], (ATOM_DIM + BOND_DIM, HIDDEN), minval=-s1, maxval=s1, dtype=jnp.float32)
        msg_b1 = jax.random.uniform(ks[4], (HIDDEN,), minval=-s1, maxval=s1, dtype=jnp.float32)
        msg_w2 = jax.random.uniform(ks[5], (HIDDEN, HIDDEN), minval=-s2, maxval=s2, dtype=jnp.float32)
        msg_b2 = jax.random.uniform(ks[6], (HIDDEN,), minval=-s2, maxval=s2, dtype=jnp.float32)
        upd_w1 = jax.random.uniform(ks[7], (ATOM_DIM + HIDDEN, HIDDEN), minval=-s3, maxval=s3, dtype=jnp.float32)
        upd_b1 = jax.random.uniform(ks[8], (HIDDEN,), minval=-s3, maxval=s3, dtype=jnp.float32)
        upd_w2 = jax.random.uniform(ks[9], (HIDDEN, HIDDEN), minval=-s2, maxval=s2, dtype=jnp.float32)
        upd_b2 = jax.random.uniform(ks[10], (HIDDEN,), minval=-s2, maxval=s2, dtype=jnp.float32)
        return {'x': x, 'edge_index': edge_index, 'edge_attr': edge_attr, 'msg_w1': msg_w1, 'msg_b1': msg_b1, 'msg_w2': msg_w2, 'msg_b2': msg_b2, 'upd_w1': upd_w1, 'upd_b1': upd_b1, 'upd_w2': upd_w2, 'upd_b2': upd_b2}
    _L0_gnn_all = _L0_gnn_setup()
    _L0_gnn_in = {k: v for k, v in _L0_gnn_all.items() if k in ('msg_w1', 'msg_b1', 'msg_w2', 'msg_b2', 'upd_w1', 'upd_b1', 'upd_w2', 'upd_b2')}
    del _L0_gnn_all
    return {'x': x, 'src': src, 'dst': dst, 'edge_attr_64': edge_attr_64, 'L0_gnn_msg_w1': _L0_gnn_in['msg_w1'], 'L0_gnn_msg_b1': _L0_gnn_in['msg_b1'], 'L0_gnn_msg_w2': _L0_gnn_in['msg_w2'], 'L0_gnn_msg_b2': _L0_gnn_in['msg_b2'], 'L0_gnn_upd_w1': _L0_gnn_in['upd_w1'], 'L0_gnn_upd_b1': _L0_gnn_in['upd_b1'], 'L0_gnn_upd_w2': _L0_gnn_in['upd_w2'], 'L0_gnn_upd_b2': _L0_gnn_in['upd_b2']}

def reference(x, src, dst, edge_attr_64, L0_gnn_msg_w1, L0_gnn_msg_b1, L0_gnn_msg_w2, L0_gnn_msg_b2, L0_gnn_upd_w1, L0_gnn_upd_b1, L0_gnn_upd_w2, L0_gnn_upd_b2):
    import jax
    import jax.numpy as jnp

    def _L0_gnn_ref(x, edge_index, edge_attr, msg_w1, msg_b1, msg_w2, msg_b2, upd_w1, upd_b1, upd_w2, upd_b2):
        import jax, jax.numpy as jnp
        import numpy as np
        N_NODES = 625
        N_EDGES = 10000
        ATOM_DIM = 128
        BOND_DIM = 64
        HIDDEN = 128
        row, col = (edge_index[0], edge_index[1])
        m_in = jnp.concatenate([x[row], edge_attr], axis=1)
        h = jax.nn.relu(m_in @ msg_w1 + msg_b1)
        messages = h @ msg_w2 + msg_b2
        aggregated = jax.ops.segment_sum(messages, col, num_segments=x.shape[0])
        u_in = jnp.concatenate([x, aggregated], axis=1)
        u = jax.nn.relu(u_in @ upd_w1 + upd_b1)
        updated_x = u @ upd_w2 + upd_b2
        return updated_x
    edge_index = jnp.stack([src, dst])
    h = jnp.maximum(_layernorm(x, axis=-1), 0.0)
    x = x + _L0_gnn_ref(h, edge_index, edge_attr_64, L0_gnn_msg_w1, L0_gnn_msg_b1, L0_gnn_msg_w2, L0_gnn_msg_b2, L0_gnn_upd_w1, L0_gnn_upd_b1, L0_gnn_upd_w2, L0_gnn_upd_b2)
    return x

_drawn_inputs = setup_inputs


def setup_inputs(seed=0):
    import zlib

    import numpy as np

    out = dict(_drawn_inputs(seed))
    spreads = {}
    factors = {'edge_attr_64': 5.706,
     'L0_gnn_msg_w1': 4.206,
     'L0_gnn_msg_b1': 8.0,
     'L0_gnn_msg_w2': 2.916,
     'L0_gnn_msg_b2': 8.0,
     'L0_gnn_upd_b1': 3.326}
    for name, (base, spread) in spreads.items():
        noise = np.random.default_rng([zlib.crc32(name.encode()), seed]).standard_normal(out[name].shape)
        drawn = base * np.exp(spread * noise) if base else spread * noise
        out[name] = jnp.asarray(drawn.astype(out[name].dtype))
    for name, factor in factors.items():
        out[name] = (out[name] * factor).astype(out[name].dtype)
    return out
```

```python
import concourse.bass as bass
from concourse import mybir
from concourse.alu_op_type import AluOpType as ALU
from contextlib import ExitStack


def bass_preln_gnn(
    nc: bass.Bass,
    x: bass.AP,
    src: bass.AP,
    dst: bass.AP,
    edge_attr: bass.AP,
    msg_w1: bass.AP,
    msg_b1: bass.AP,
    msg_w2: bass.AP,
    msg_b2: bass.AP,
    upd_w1: bass.AP,
    upd_b1: bass.AP,
    upd_w2: bass.AP,
    upd_b2: bass.AP,
    out: bass.AP,
):
    f32 = mybir.dt.float32
    bf16 = mybir.dt.bfloat16
    i32 = mybir.dt.int32
    ACT = mybir.ActivationFunctionType
    AX = mybir.AxisListType

    NODES, D = x.shape
    EDGES, DE = edge_attr.shape
    EPS = 1e-5
    P = 128
    T = 16
    GN = P * T
    C = 4
    GE = P * C
    Q = T // 4
    G = -(-NODES // GN)
    LAST = G - 1
    assert G == -(-EDGES // GE)
    NODE_LAST = NODES - GN
    EDGE_LAST = EDGES - GE
    CARRY_LAST = EDGE_LAST - 1 - (LAST - 1) * GE
    FAR = 1 << 20
    SQD = float(D) ** 0.5
    NT = T + 2 * C

    LN = 12
    SB = 10
    SW = EDGES // SB
    FLAT = 4 * SW + (4 + SB) * GE + 2
    assert SW * SB == EDGES

    ctx = ExitStack()
    with ctx:
        def sb(name, shape, dt=f32):
            return ctx.enter_context(nc.sbuf_tensor(name, shape, dt))

        def ps(name):
            return ctx.enter_context(nc.psum_tensor(name, [P, 512], f32))

        def sem(name):
            return ctx.enter_context(nc.semaphore(name))

        mask_dram = nc.dram_tensor("mask_dram", [G, GE], bf16, kind="Internal").ap()
        src_sorted = nc.dram_tensor("src_sorted", [EDGES, 1], i32, kind="Internal").ap()
        dst_sorted = nc.dram_tensor("dst_sorted", [EDGES, 1], i32, kind="Internal").ap()
        erow_dram = nc.dram_tensor("erow_dram", [G * GE, D], f32, kind="Internal").ap()
        attr_sorted = nc.dram_tensor("attr_sorted", [EDGES, DE], f32, kind="Internal").ap()

        W1a, W1b = sb("W1a", [D, D]), sb("W1b", [DE, D])
        W2, W2T, U1b, V = sb("W2", [D, D]), sb("W2T", [D, D]), sb("U1b", [D, D]), sb("V", [D, D])
        U1a, U2 = sb("U1a", [D, D]), sb("U2", [D, D])
        b1, b2, c1, vb = sb("b1", [D, 1]), sb("b2", [D, 1]), sb("c1", [D, 1]), sb("vb", [D, 1])
        c2 = sb("c2", [P, D])
        ident = sb("ident", [P, P])
        ones = sb("ones", [P, 1])
        pad = sb("pad", [1, 1])

        xin = [sb(f"xin{s}", [P, T, D]) for s in range(2)]
        y = [sb(f"y{s}", [P, T, D]) for s in range(2)]
        xo = [sb(f"xo{s}", [P, T, D]) for s in range(2)]
        hT = [sb(f"hT{s}", [D, 512]) for s in range(2)]
        uT = [sb(f"uT{q}", [D, 4, P]) for q in range(Q)]

        xs = [sb(f"xs{s}", [P, C, D]) for s in range(2)]
        xd = [sb(f"xd{s}", [P, C, D]) for s in range(2)]
        ys = [sb(f"ys{s}", [P, C, D]) for s in range(2)]
        yd = [sb(f"yd{s}", [P, C, D]) for s in range(2)]
        ea = [sb(f"ea{s}", [P, C, DE]) for s in range(2)]
        mask = [sb(f"mask{s}", [P, GE], bf16) for s in range(2)]
        run = [sb(f"run{s}", [D, GE]) for s in range(2)]
        hsT, hdT, eaT = sb("hsT", [D, GE]), sb("hdT", [D, GE]), sb("eaT", [DE, GE])
        zT, mT, preT, ueT = sb("zT", [D, GE]), sb("mT", [D, GE]), sb("preT", [D, GE]), sb("ueT", [D, C, P])
        erow = [sb(f"erow{s}", [P, C, D]) for s in range(2)]
        flat = sb("flat", [G, FLAT])

        st = sb("st", [P, NT, 6])
        st_sum, st_dif = sb("st_sum", [P, NT]), sb("st_dif", [P, NT])
        st_q, st_dd, st_v = sb("st_q", [P, NT]), sb("st_dd", [P, NT]), sb("st_v", [P, NT])
        st_root, st_r = sb("st_root", [P, NT]), sb("st_r", [P, NT])
        mean = [sb(f"mean{s}", [P, NT]) for s in range(2)]
        rstd = [sb(f"rstd{s}", [P, NT]) for s in range(2)]
        shift = [sb(f"shift{s}", [P, NT]) for s in range(2)]

        DEXT = FLAT - GE - 2
        dext = flat[0:G, DEXT:DEXT + GE + 2].bitcast(i32)
        d_prev, d_cur, d_next = dext[:, 0:GE], dext[:, 1:GE + 1], dext[:, 2:GE + 2]
        srow = ueT[0:G, :, :].rearrange("g c p -> g (c p)").bitcast(i32)
        gidx = sb("gidx", [G, 1], i32)
        bound = sb("bound", [G, 1])
        lastg = sb("lastg", [G, 1])
        far_flag = sb("far_flag", [G, 1])
        sf, df, wf = hsT[0:G, :], hdT[0:G, :], zT[0:G, :]
        same_next, bad = mT[0:G, :], preT[0:G, :]
        bad_sum = sb("bad_sum", [G, 2])
        mrow = sb("mrow", [G, GE], bf16)
        src_idx, dst_idx, out_idx = (sb(n, [P, G, C], i32) for n in ("src_idx", "dst_idx", "out_idx"))
        g_idx = [sb(f"g_idx{s}", [P, 2, C], i32) for s in range(2)]
        o_idx = [sb(f"o_idx{s}", [P, C], i32) for s in range(2)]
        rank_col, src_col, dst_col = (o_idx[0][0:G, n:n + 1] for n in range(3))
        flags = sb("flags", [1, 2], i32)

        bT = [ps("bT0"), ps("bT1")]
        bP = [ps("bP0"), ps("bP1")]
        PB = [0, 0, 0, 1]
        bO = [ps("bO0"), ps("bO1")]
        bM, bE = ps("bM"), ps("bE")

        s_x = [sem(f"s_x{s}") for s in range(2)]
        s_ea = [sem(f"s_ea{s}") for s in range(2)]
        s_src = [sem(f"s_src{s}") for s in range(2)]
        s_store = [sem(f"s_store{s}") for s in range(2)]
        s_erow = [sem(f"s_erow{s}") for s in range(2)]
        s_scat, s_back = sem("s_scat"), sem("s_back")
        s_w, s_dext, s_srow, s_mstore = sem("s_w"), sem("s_dext"), sem("s_srow"), sem("s_mstore")
        s_fill, s_ident, s_iota = sem("s_fill"), sem("s_ident"), sem("s_iota")
        s_idc, s_bad = sem("s_idc"), sem("s_bad")
        s_sorted_keys = sem("s_sorted_keys")
        s_flag_ps, s_flag = sem("s_flag_ps"), sem("s_flag")
        s_mrow, s_idf, s_idx_ps, s_idx = sem("s_mrow"), sem("s_idf"), sem("s_idx_ps"), sem("s_idx")
        s_w2t_ps, s_w2t, s_v_ps, s_v = sem("s_w2t_ps"), sem("s_w2t"), sem("s_v_ps"), sem("s_v")
        s_ln = sem("s_ln")
        s_root = sem("s_root")
        s_tiles_stats = sem("s_tiles_stats")
        s_y = sem("s_y")
        s_ye = sem("s_ye")
        s_xo, s_rows = sem("s_xo"), sem("s_rows")
        p_hT, p_ea, p_hs, p_hd = sem("p_hT"), sem("p_ea"), sem("p_hs"), sem("p_hd")
        p_pre, p_z, p_m, p_pree, p_out, p_oute = (sem(n) for n in ("p_pre", "p_z", "p_m", "p_pree", "p_out", "p_oute"))
        a_hT, a_ea, a_hs, a_hd, a_u, a_z, a_m, a_ue = (sem(n) for n in ("a_hT", "a_ea", "a_hs", "a_hd", "a_u", "a_z", "a_m", "a_ue"))
        v_run, v_pree, v_out, v_oute = sem("v_run"), sem("v_pree"), sem("v_out"), sem("v_oute")
        v_init = sem("v_init")
        r_blk, r_step, r_rank, r_row, r_scat, r_dma = (sem(n) for n in ("r_blk", "r_step", "r_rank", "r_row", "r_scat", "r_dma"))
        r_iota, r_col = sem("r_iota"), sem("r_col")
        s_gi, s_oi = sem("s_gi"), sem("s_oi")

        dst_blk = flat[0:G, 0:SW].bitcast(i32)
        pos_blk = flat[0:G, SW:2 * SW]
        cmp_a, cmp_b = flat[0:G, 2 * SW:3 * SW], flat[0:G, 3 * SW:4 * SW]
        base_f = 4 * SW
        own = flat[0:G, base_f:base_f + GE]
        own_b = flat[0:G, base_f + GE:base_f + 2 * GE]
        part = flat[0:G, base_f + 2 * GE:base_f + 2 * GE + SB * GE].rearrange("p (b c) -> p b c", b=SB)
        rank = flat[0:G, base_f + (2 + SB) * GE:base_f + (3 + SB) * GE].bitcast(i32)
        attr_row = cmp_a[:, 0:DE]

        def wait(eng, s, count):
            if not (isinstance(count, int) and count <= 0):
                eng.wait_ge(s, count)

        def node_rows(t, base):
            return t[bass.ds(base, GN), :].rearrange("(p t) d -> p t d", t=T)

        def attr_rows(t, base):
            return t[bass.ds(base, GE), :].rearrange("(p c) d -> p c d", c=C)

        def col(v):
            return v.rearrange("(n a) -> n a", a=1)

        block = ctx.enter_context(nc.Block())

        @block.sync
        def _(sp):
            def load_x(base, s):
                sp.dma_start(xin[s][:, :, :], node_rows(x, base)).then_inc(s_x[s], 16)

            def load_keys(d):
                mid = bass.AP(tensor=d.tensor, offset=d.offset + GE - 1, ap=[[GE, LAST - 1], [1, GE + 2]])
                sp.dma_start(dext[1:LAST, :], mid).then_inc(s_dext, 16)
                sp.dma_start(dext[0:1, 1:GE + 2], d[0:GE + 1].rearrange("(a n) -> a n", a=1)).then_inc(s_dext, 16)
                sp.dma_start(dext[LAST:G, 0:GE + 1], d[EDGE_LAST - 1:EDGES].rearrange("(a n) -> a n", a=1)).then_inc(s_dext, 16)

            def load_src(v):
                sp.dma_start(srow[0:LAST, :], v[0:LAST * GE].rearrange("(g n) -> g n", n=GE)).then_inc(s_srow, 16)
                sp.dma_start(srow[LAST:G, :], v[EDGE_LAST:EDGES].rearrange("(g n) -> g n", n=GE)).then_inc(s_srow, 16)

            sp.wait_ge(s_fill, 2)
            load_keys(dst)
            load_x(0, 0)
            load_src(src)
            for t, v in ((W1a, msg_w1[0:D, :]), (W1b, msg_w1[D:D + DE, :]), (W2, msg_w2), (U1a, upd_w1[0:D, :]),
                         (U1b, upd_w1[D:2 * D, :]), (U2, upd_w2), (b1, col(msg_b1)), (b2, col(msg_b2)),
                         (c1, col(upd_b1)), (c2, upd_b2.partition_broadcast(P))):
                sp.dma_start(t[:, :], v).then_inc(s_w, 16)
            load_x(GN, 1)

            sp.wait_ge(s_flag, 1)
            unsorted = sp.value_load(flags[0:1, 0:1])
            with sp.If(unsorted != 0):
                for b in range(SB):
                    if b:
                        sp.wait_ge(r_step, 4 * GE * b)
                    sp.dma_start(dst_blk, dst[b * SW:(b + 1) * SW].partition_broadcast(G)).then_inc(r_blk, 16)
                sp.wait_ge(r_rank, 1)

                def attr_column(c):
                    rest = edge_attr[0:LAST * GE, :].rearrange("(g n) d -> g n d", n=GE)[:, c, :]
                    sp.dma_start(attr_row[0:LAST, :], rest).then_inc(r_row, 16)
                    sp.dma_start(attr_row[LAST:G, :], edge_attr[bass.ds(c + EDGE_LAST, 1), :]).then_inc(r_row, 16)

                attr_column(0)
                with sp.Fori(1, GE) as c:
                    sp.wait_ge(r_scat, c * 48)
                    attr_column(c)
                sp.wait_ge(r_scat, GE * 48)
                load_keys(dst_sorted.rearrange("n a -> (n a)"))
                load_src(src_sorted.rearrange("n a -> (n a)"))
                sp.wait_ge(s_dext, 96)
                sp.wait_ge(s_srow, 64)
            sp.wait_ge(s_dext, 48)
            sp.wait_ge(s_srow, 32)
            sp.sem_inc(s_sorted_keys, 1)

            sp.wait_ge(s_mrow, 1)
            sp.dma_start(mask_dram, mrow[:, :]).then_inc(s_mstore, 16)
            sp.wait_ge(s_mstore, 16)

            def load_edges(g, base, s):
                m = mask_dram[bass.ds(g, 1), :].rearrange("a n -> (a n)")
                sp.dma_start(mask[s][:, :], m.partition_broadcast(P)).then_inc(s_ea[s], 16)
                with sp.If(unsorted != 0):
                    sp.dma_start(ea[s][:, :, :], attr_rows(attr_sorted, base)).then_inc(s_ea[s], 16)
                with sp.If(unsorted == 0):
                    sp.dma_start(ea[s][:, :, :], attr_rows(edge_attr, base)).then_inc(s_ea[s], 16)

            load_edges(0, 0, 0)
            load_edges(1, GE, 1)

            def step(g, s, nbase, ebase):
                if nbase is not None:
                    sp.wait_ge(s_y, Q * (g + 1))
                    sp.wait_ge(s_xo, g + 1)
                    load_x(nbase, s)
                    sp.wait_ge(p_ea, g + 1)
                    sp.wait_ge(v_run, g + 1)
                    load_edges(g + 2, ebase, s)
                sp.wait_ge(v_out, Q * (g + 1))
                if isinstance(g, int) and g == LAST:
                    sp.wait_ge(s_store[1 - s], 16 * (LAST // 2))
                    sp.dma_start(node_rows(out, NODE_LAST), xo[s][:, :, :]).then_inc(s_store[s], 16)
                else:
                    sp.dma_start(node_rows(out, g * GN), xo[s][:, :, :]).then_inc(s_store[s], 16)

            with sp.Fori(0, LAST // 2 - 1) as i:
                for s in range(2):
                    g = 2 * i + s
                    step(g, s, (g + 2) * GN, (g + 2) * GE)
            step(LAST - 2, 0, NODE_LAST, EDGE_LAST)
            step(LAST - 1, 1, None, None)
            step(LAST, 0, None, None)
            sp.wait_ge(s_store[0], 16 * (LAST // 2 + 1))
            sp.wait_ge(s_store[1], 16 * (LAST // 2))

        @block.gpsimd
        def _(pool):
            def carry_wait():
                pool.tensor_tensor(out=pad[:, :], in0=ident[0:1, 0:1], in1=ident[0:1, 0:1], op=ALU.add)

            pool.memset(dext[:, 0:1], -1).then_inc(s_fill, 1)
            pool.memset(dext[:, GE + 1:GE + 2], FAR).then_inc(s_fill, 1)
            pool.iota(gidx[:, :], pattern=[[0, 1]], base=0, channel_multiplier=1).then_inc(s_iota, 1)
            pool.memset(ident[:, :], 0.0).then_inc(s_ident, 1)
            pool.memset(ones[:, :], 1.0).then_inc(s_ident, 1)
            pool.wait_ge(s_ident, 2)
            pool.affine_select(out=ident[:, :], in_=ident[:, :], compare_op=ALU.not_equal, fill=1.0,
                               base=0, pattern=[[-1, P]], channel_multiplier=1).then_inc(s_ident, 1)
            pool.wait_ge(s_ident, 3)

            pool.wait_ge(s_flag, 1)
            unsorted = pool.value_load(flags[0:1, 0:1])
            with pool.If(unsorted != 0):
                pool.iota(pos_blk, pattern=[[1, SW]], base=0, channel_multiplier=0,
                          allow_small_or_imprecise_dtypes=True).then_inc(r_iota, 1)
                pool.iota(own[0:G, :], pattern=[[1, GE]], base=0, channel_multiplier=GE,
                          allow_small_or_imprecise_dtypes=True).then_inc(r_iota, 1)
                pool.wait_ge(r_rank, 1)
                pool.wait_ge(s_srow, 32)
                with pool.Fori(0, GE) as c:
                    pool.wait_ge(r_row, (c + 1) * 32)
                    pool.tensor_copy(rank_col, rank[:, bass.ds(c, 1)]).then_inc(r_col, 1)
                    pool.tensor_copy(src_col, srow[:, bass.ds(c, 1)]).then_inc(r_col, 1)
                    pool.tensor_copy(dst_col, dext[:, bass.ds(c + 1, 1)]).then_inc(r_col, 1)
                    pool.wait_ge(r_col, 3 * (c + 1))
                    carry_wait()
                    off = bass.IndirectOffsetOnAxis(rank_col, 0)
                    pool.indirect_dma_start(attr_sorted, off, attr_row, None).then_inc(r_scat, 16)
                    pool.indirect_dma_start(src_sorted, off, src_col, None).then_inc(r_scat, 16)
                    pool.indirect_dma_start(dst_sorted, off, dst_col, None).then_inc(r_scat, 16)
                    pool.wait_ge(r_scat, (c + 1) * 48)
                    carry_wait()
            pool.wait_ge(s_flag, 2)
            late = pool.value_load(flags[0:1, 1:2])
            pool.wait_ge(s_idx, 3)

            def indices(g, s):
                pool.tensor_copy(g_idx[s][:, 0, :], src_idx[:, g, :]).then_inc(s_gi, 1)
                pool.tensor_copy(g_idx[s][:, 1, :], dst_idx[:, g, :]).then_inc(s_gi, 1)

            def gather(s):
                for n, t in enumerate((xs[s], xd[s])):
                    for c in range(C):
                        pool.indirect_dma_start(t[:, c, :], None, x,
                                                bass.IndirectOffsetOnAxis(g_idx[s][:, n, c:c + 1], 0)).then_inc(s_src[s], 16)

            def row_indices(g, s):
                pool.tensor_copy(o_idx[s][:, :], out_idx[:, g, :]).then_inc(s_oi, 1)
                pool.wait_ge(s_oi, g + 1)
                carry_wait()

            def scatter(s, done):
                for c in range(C):
                    pool.indirect_dma_start(out, bass.IndirectOffsetOnAxis(o_idx[s][:, c:c + 1], 0),
                                            erow[s][:, c, :], None,
                                            bounds_check=NODES - 1, oob_is_err=False).then_inc(done, 16)

            def c2_rows(n):
                return c2[:, :].rearrange("p (a d) -> p a d", a=1).to_broadcast([P, n, D])

            def node_residual(s, n):
                pool.wait_ge(s_x[s], 16 * n)
                wait(pool, s_store[s], 16 * (n - 1))
                pool.tensor_tensor(out=xo[s][:, :, :], in0=xin[s][:, :, :], in1=c2_rows(T), op=ALU.add).then_inc(s_xo, 1)

            def edge_residual(s, n):
                pool.wait_ge(s_src[s], 2 * C * 16 * n)
                wait(pool, s_erow[s], C * 16 * (n - 1))
                pool.tensor_tensor(out=erow[s][:, :, :], in0=xd[s][:, :, :], in1=c2_rows(C), op=ALU.add).then_inc(s_rows, 1)

            pool.wait_ge(s_w, 160)
            indices(0, 0)
            indices(1, 1)
            pool.wait_ge(s_gi, 4)
            gather(0)
            gather(1)
            node_residual(0, 1)
            edge_residual(0, 1)

            def step(g, s, gather_next, n_next, n_prev):
                if gather_next:
                    indices(g + 2, s)
                    pool.wait_ge(s_gi, 2 * g + 6)
                    pool.wait_ge(s_ye, 2 * (g + 1))
                    pool.wait_ge(s_rows, g + 1)
                    carry_wait()
                    gather(s)
                if n_prev is not None:
                    pool.wait_ge(v_oute, g)
                    pool.wait_ge(s_store[1 - s], 16 * n_prev)
                    row_indices(g - 1, 1 - s)
                    with pool.If(late == 0):
                        scatter(1 - s, s_erow[1 - s])
                    with pool.If(late != 0):
                        for c in range(C):
                            pool.dma_start(erow_dram[bass.ds((g - 1) * GE + c * P, P), :],
                                           erow[1 - s][:, c, :]).then_inc(s_erow[1 - s], 16)
                if n_next is not None:
                    node_residual(1 - s, n_next)
                    edge_residual(1 - s, n_next)

            step(0, 0, True, 1, None)
            step(1, 1, True, 2, 1)
            with pool.Fori(1, LAST // 2 - 1) as i:
                step(2 * i, 0, True, i + 1, i)
                step(2 * i + 1, 1, True, i + 2, i + 1)
            step(LAST - 2, 0, True, LAST // 2, LAST // 2 - 1)
            step(LAST - 1, 1, False, LAST // 2 + 1, LAST // 2)
            step(LAST, 0, False, None, LAST // 2)
            pool.wait_ge(v_oute, G)
            pool.wait_ge(s_store[0], 16 * (LAST // 2 + 1))
            pool.wait_ge(s_store[1], 16 * (LAST // 2))
            row_indices(LAST, 0)
            pool.wait_ge(s_erow[0], C * 16 * (LAST // 2))
            pool.wait_ge(s_erow[1], C * 16 * (LAST // 2))
            scatter(0, s_scat)
            pool.wait_ge(s_scat, 16 * C)
            with pool.If(late != 0):
                with pool.Fori(0, LAST) as g:
                    pool.tensor_copy(o_idx[0][:, :], out_idx[:, g, :]).then_inc(s_oi, 1)
                    for c in range(C):
                        pool.dma_start(erow[0][:, c, :], erow_dram[bass.ds(g * GE + c * P, P), :]).then_inc(s_back, 16)
                    pool.wait_ge(s_back, 16 * C * (g + 1))
                    pool.wait_ge(s_oi, G + g + 1)
                    carry_wait()
                    scatter(0, s_scat)
                    pool.wait_ge(s_scat, 16 * C * (g + 2))
                    carry_wait()

        @block.scalar
        def _(act):
            def relu_scaled(o, i):
                return nc.scalar.activation(o, i, ACT.Relu, scale=SQD)

            def norm_edges(g1, s, js):
                for j in js:
                    t, tile, k = (xs, ys, j) if j < C else (xd, yd, j - C)
                    last = nc.scalar.activation(tile[s][:, k, :], t[s][:, k, :], ACT.Identity,
                                                scale=rstd[s][:, T + j:T + j + 1], bias=shift[s][:, T + j:T + j + 1])
                    if k == C - 1:
                        last.then_inc(s_ye, 1)

            act.wait_ge(s_w2t_ps, 1)
            nc.scalar.activation(W2T[:, :], bM[:, 0:D], ACT.Copy).then_inc(s_w2t, 1)
            act.wait_ge(s_v_ps, 1)
            nc.scalar.activation(V[:, :], bE[:, 0:D], ACT.Copy).then_inc(s_v, 1)
            nc.scalar.activation(vb[:, :], bE[:, D:D + 1], ACT.Copy).then_inc(s_v, 1)
            act.wait_ge(s_v, 2)
            act.wait_ge(s_w, 160)

            def root(g):
                act.wait_ge(s_ln, LN * g + 7)
                nc.scalar.activation(st_root[:, :], st_v[:, :], ACT.Sqrt).then_inc(s_root, 1)

            root(0)
            act.wait_ge(p_hT, 1)
            relu_scaled(hT[0][:, :], bT[0][:, :]).then_inc(a_hT, 1)
            act.wait_ge(s_ln, LN)
            norm_edges(0, 0, range(2 * C))

            def evac_u(g, k):
                act.wait_ge(p_pre, Q * g + k + 1)
                nc.scalar.activation(uT[k][:, :, :].rearrange("d c p -> d (c p)"), bP[PB[k]][:, :], ACT.Relu,
                                     bias=c1[:, 0:1]).then_inc(a_u, 1)

            def group(g, s, more):
                act.wait_ge(p_hT, Q * g + 2)
                relu_scaled(hT[1][:, :], bT[1][:, :]).then_inc(a_hT, 1)
                act.wait_ge(p_ea, g + 1)
                nc.scalar.activation(eaT[:, :], bM[0:DE, :], ACT.Copy).then_inc(a_ea, 1)
                act.wait_ge(p_hs, g + 1)
                relu_scaled(hsT[:, :], bT[0][:, :]).then_inc(a_hs, 1)
                evac_u(g, 0)
                act.wait_ge(p_hT, Q * g + 3)
                relu_scaled(hT[0][:, :], bT[1][:, :]).then_inc(a_hT, 1)
                act.wait_ge(p_z, g + 1)
                nc.scalar.activation(zT[:, :], bP[1][:, :], ACT.Relu, bias=b1[:, 0:1]).then_inc(a_z, 1)
                evac_u(g, 1)
                act.wait_ge(p_hd, g + 1)
                relu_scaled(hdT[:, :], bT[0][:, :]).then_inc(a_hd, 1)
                act.wait_ge(p_m, g + 1)
                wait(act, v_run, g)
                nc.scalar.activation(mT[:, :].rearrange("d (p c) -> d c p", c=C),
                                     bM[:, :].rearrange("d (c p) -> d c p", c=C), ACT.Identity,
                                     bias=vb[:, 0:1]).then_inc(a_m, 1)
                if more:
                    root(g + 1)
                act.wait_ge(p_hT, Q * g + 4)
                relu_scaled(hT[1][:, :], bT[1][:, :]).then_inc(a_hT, 1)
                evac_u(g, 2)
                act.wait_ge(v_pree, g + 1)
                nc.scalar.activation(ueT[:, :, :].rearrange("d c p -> d (c p)"), preT[:, :], ACT.Relu,
                                     bias=c1[:, 0:1]).then_inc(a_ue, 1)
                if more:
                    act.wait_ge(s_ln, LN * (g + 2))
                    norm_edges(g + 1, 1 - s, range(0, 4))
                evac_u(g, 3)
                if more:
                    norm_edges(g + 1, 1 - s, range(4, 8))
                    act.wait_ge(p_hT, Q * g + 5)
                    relu_scaled(hT[0][:, :], bT[0][:, :]).then_inc(a_hT, 1)

            group(0, 0, True)
            group(1, 1, True)
            with act.Fori(1, LAST // 2) as i:
                group(2 * i, 0, True)
                group(2 * i + 1, 1, True)
            group(LAST, 0, False)

        @block.vector
        def _(dve):
            nc.vector.memset(run[1][:, :], 0.0).then_inc(v_init, 1)

            def stats(s, js):
                for j in js:
                    t, k = (xin, j) if j < T else (xs, j - T) if j < T + C else (xd, j - T - C)
                    last = nc.vector.bn_stats(st[:, j, :], t[s][:, k, :])
                return last

            dve.wait_ge(s_dext, 48)
            dve.wait_ge(s_fill, 2)
            nc.vector.tensor_tensor(out=bad[:, :], in0=d_cur, in1=d_next, op=ALU.is_gt).then_inc(s_idc, 1)
            dve.wait_ge(s_idc, 1)
            nc.vector.reduce_sum(bad_sum[:, 0:1], bad[:, :], axis=AX.X).then_inc(s_bad, 1)
            dve.wait_ge(s_flag_ps, 1)
            nc.vector.tensor_copy(flags[0:1, 0:1], bE[0:1, 0:1]).then_inc(s_flag, 1)

            dve.wait_ge(s_flag, 1)
            unsorted = dve.value_load(flags[0:1, 0:1])
            with dve.If(unsorted != 0):
                dve.wait_ge(r_iota, 2)
                nc.vector.tensor_copy(df[:, :], d_cur).then_inc(r_dma, 1)
                for b in range(SB):
                    dve.wait_ge(r_blk, 16 * (b + 1))
                    nc.vector.tensor_scalar(own_b, own, float(b * SW), None, ALU.subtract).then_inc(r_dma, 1)
                    dve.wait_ge(r_dma, b + 2)
                    def count_column(c):
                        n = c * 4 + b * 4 * GE
                        wait(dve, r_step, n)
                        nc.vector.tensor_scalar(cmp_a, dst_blk, df[:, bass.ds(c, 1)], 32768.0, ALU.subtract, ALU.mult).then_inc(r_step, 1)
                        dve.wait_ge(r_step, n + 1)
                        nc.vector.scalar_tensor_tensor(out=cmp_b, in0=cmp_a, scalar=own_b[:, bass.ds(c, 1)], in1=pos_blk,
                                                       op0=ALU.subtract, op1=ALU.add).then_inc(r_step, 1)
                        dve.wait_ge(r_step, n + 2)
                        nc.vector.tensor_scalar(cmp_a, cmp_b, 0.0, None, ALU.is_lt).then_inc(r_step, 1)
                        dve.wait_ge(r_step, n + 3)
                        nc.vector.reduce_sum(part[:, b, bass.ds(c, 1)], cmp_a, axis=AX.X).then_inc(r_step, 1)

                    count_column(0)
                    with dve.Fori(1, GE) as c:
                        count_column(c)
                    dve.wait_ge(r_step, (b + 1) * 4 * GE)
                nc.vector.reduce_sum(own_b, part.rearrange("p b c -> p c b"), axis=AX.X).then_inc(r_dma, 1)
                dve.wait_ge(r_dma, SB + 2)
                nc.vector.tensor_copy(rank, own_b).then_inc(r_rank, 1)

            dve.wait_ge(s_sorted_keys, 1)
            dve.wait_ge(s_iota, 1)
            V_ = nc.vector
            V_.tensor_tensor(out=mrow[:, :], in0=d_cur, in1=d_prev, op=ALU.is_equal).then_inc(s_mrow, 1)
            V_.tensor_tensor(out=same_next[:, :], in0=d_cur, in1=d_next, op=ALU.is_equal).then_inc(s_idc, 1)
            V_.tensor_copy(df[:, :], d_cur).then_inc(s_idf, 1)
            V_.tensor_copy(sf[:, :], srow[:, :]).then_inc(s_idf, 1)
            V_.tensor_scalar(bound[:, :], gidx[:, :], float(GN), float(GN), ALU.mult, ALU.add).then_inc(s_idc, 1)
            V_.tensor_scalar(lastg[:, :], gidx[:, :], float(LAST), float(FAR), ALU.is_equal, ALU.mult).then_inc(s_idc, 1)
            dve.wait_ge(s_idc, 4)
            V_.tensor_scalar(bound[:, :], bound[:, :], float(NODE_LAST), lastg[:, 0:1], ALU.min, ALU.add).then_inc(s_idc, 1)
            dve.wait_ge(s_idf, 2)
            V_.scalar_tensor_tensor(out=wf[:, :], in0=same_next[:, :], scalar=float(FAR), in1=df[:, :],
                                    op0=ALU.mult, op1=ALU.add).then_inc(s_idf, 1)
            dve.wait_ge(s_idc, 5)
            V_.tensor_scalar(bad[:, :], df[:, :], bound[:, 0:1], None, ALU.is_ge).then_inc(s_idc, 1)
            dve.wait_ge(s_idc, 6)
            V_.reduce_sum(bad_sum[:, 1:2], bad[:, :], axis=AX.X).then_inc(s_bad, 1)
            for n, (t, bank) in enumerate(((src_idx, bT[0]), (dst_idx, bT[1]), (out_idx, bP[0]))):
                dve.wait_ge(s_idx_ps, n + 1)
                V_.tensor_copy(t[:, :, :].rearrange("p g c -> p c g"),
                               bank[:, 0:C * G].rearrange("p (c g) -> p c g", c=C)).then_inc(s_idx, 1)
            dve.wait_ge(s_flag_ps, 2)
            V_.tensor_copy(flags[0:1, 1:2], bE[0:1, 256:257]).then_inc(s_flag, 1)

            def ln_variance(g, s):
                n = LN * g
                dve.wait_ge(s_tiles_stats, 2 * (g + 1))
                V_.tensor_tensor(out=st_dif[:, :], in0=st[:, :, 1], in1=st[:, :, 4], op=ALU.subtract).then_inc(s_ln, 1)
                V_.tensor_tensor(out=st_q[:, :], in0=st[:, :, 2], in1=st[:, :, 5], op=ALU.add).then_inc(s_ln, 1)
                V_.tensor_tensor(out=st_sum[:, :], in0=st[:, :, 1], in1=st[:, :, 4], op=ALU.add).then_inc(s_ln, 1)
                dve.wait_ge(s_ln, n + 1)
                V_.tensor_tensor(out=st_dd[:, :], in0=st_dif[:, :], in1=st_dif[:, :], op=ALU.mult).then_inc(s_ln, 1)
                dve.wait_ge(s_ln, n + 3)
                V_.tensor_scalar(mean[s][:, :], st_sum[:, :], 0.5, None, ALU.mult).then_inc(s_ln, 1)
                dve.wait_ge(s_ln, n + 4)
                V_.scalar_tensor_tensor(out=st_v[:, :], in0=st_dd[:, :], scalar=float(D) / 4, in1=st_q[:, :],
                                        op0=ALU.mult, op1=ALU.add).then_inc(s_ln, 1)
                dve.wait_ge(s_ln, n + 6)
                V_.tensor_scalar(st_v[:, :], st_v[:, :], float(D) * EPS, None, ALU.add).then_inc(s_ln, 1)

            def ln_rstd(g, s):
                n = LN * g + 7
                dve.wait_ge(s_root, g + 1)
                V_.reciprocal(st_r[:, :], st_root[:, :]).then_inc(s_ln, 1)
                dve.wait_ge(s_ln, n + 1)
                V_.scalar_tensor_tensor(out=st_dd[:, :], in0=st_r[:, :], scalar=-0.5, in1=st_r[:, :],
                                        op0=ALU.mult, op1=ALU.mult).then_inc(s_ln, 1)
                dve.wait_ge(s_ln, n + 2)
                V_.tensor_tensor(out=st_q[:, :], in0=st_dd[:, :], in1=st_v[:, :], op=ALU.mult).then_inc(s_ln, 1)
                dve.wait_ge(s_ln, n + 3)
                V_.scalar_tensor_tensor(out=rstd[s][:, :], in0=st_q[:, :], scalar=1.5, in1=st_r[:, :],
                                        op0=ALU.add, op1=ALU.mult).then_inc(s_ln, 1)
                dve.wait_ge(s_ln, n + 4)
                V_.scalar_tensor_tensor(out=shift[s][:, :], in0=mean[s][:, :], scalar=-1.0, in1=rstd[s][:, :],
                                        op0=ALU.mult, op1=ALU.mult).then_inc(s_ln, 1)

            def norm(g, s, q):
                dve.wait_ge(s_ln, LN * (g + 1) - 1)
                for k in range(4 * q, 4 * q + 4):
                    last = V_.tensor_scalar(y[s][:, k, :], xin[s][:, k, :], mean[s][:, k:k + 1], rstd[s][:, k:k + 1],
                                            ALU.subtract, ALU.mult)
                last.then_inc(s_y, 1)

            dve.wait_ge(s_x[0], 16)
            stats(0, range(T)).then_inc(s_tiles_stats, 1)
            dve.wait_ge(s_src[0], 2 * C * 16)
            stats(0, range(T, NT)).then_inc(s_tiles_stats, 1)
            ln_variance(0, 0)
            ln_rstd(0, 0)
            for q in range(Q):
                norm(0, 0, q)

            def add_out(g, s, q):
                dve.wait_ge(p_out, Q * g + q + 1)
                if q == 0:
                    dve.wait_ge(s_xo, g + 1)
                o = xo[s][:, 4 * q:4 * q + 4, :].rearrange("p t d -> p (t d)")
                V_.tensor_tensor(out=o, in0=bO[q % 2][:, :], in1=o, op=ALU.add).then_inc(v_out, 1)

            def group(g, s, n, more):
                if more:
                    n_next = n + s
                    dve.wait_ge(s_x[1 - s], 16 * n_next)
                    dve.wait_ge(s_ln, LN * (g + 1))
                    stats(1 - s, range(T)).then_inc(s_tiles_stats, 1)
                    dve.wait_ge(s_src[1 - s], 2 * C * 16 * n_next)
                    stats(1 - s, range(T, NT)).then_inc(s_tiles_stats, 1)
                    wait(dve, s_ye, 2 * g)
                    wait(dve, s_y, Q * g)
                    ln_variance(g + 1, 1 - s)
                add_out(g, s, 0)
                dve.wait_ge(a_m, g + 1)
                wait(dve, v_run, g)
                dve.wait_ge(s_ea[s], 32 * n)
                last_col = CARRY_LAST if isinstance(g, int) and g == LAST else GE - 1
                V_.tensor_tensor_scan(run[s][:, :], mask[s][:, :], mT[:, :], run[1 - s][:, last_col:last_col + 1],
                                      ALU.mult, ALU.add).then_inc(v_run, 1)
                if more:
                    ln_rstd(g + 1, 1 - s)
                    wait(dve, p_hT, Q * g)
                    norm(g + 1, 1 - s, 0)
                dve.wait_ge(p_pree, g + 1)
                dve.wait_ge(v_run, g + 1)
                wait(dve, a_ue, g)
                V_.tensor_tensor(out=preT[:, :].rearrange("d (c p) -> d c p", c=C),
                                 in0=bP[1][:, :].rearrange("d (c p) -> d c p", c=C),
                                 in1=run[s][:, :].rearrange("d (p c) -> d c p", c=C), op=ALU.add).then_inc(v_pree, 1)
                add_out(g, s, 1)
                if more:
                    for q in range(1, Q):
                        norm(g + 1, 1 - s, q)
                add_out(g, s, 2)
                dve.wait_ge(p_oute, g + 1)
                dve.wait_ge(s_rows, g + 1)
                o = erow[s][:, :, :]
                V_.tensor_tensor(out=o, in0=bE[:, :].rearrange("p (c d) -> p c d", c=C), in1=o, op=ALU.add).then_inc(v_oute, 1)
                add_out(g, s, 3)

            dve.wait_ge(v_init, 1)
            group(0, 0, 1, True)
            group(1, 1, 1, True)
            with dve.Fori(1, LAST // 2) as i:
                group(2 * i, 0, i + 1, True)
                group(2 * i + 1, 1, i + 1, True)
            group(LAST, 0, LAST // 2 + 1, False)

        @block.tensor
        def _(pe):
            mm = nc.tensor.matmul
            pe.wait_ge(s_ident, 3)
            pe.wait_ge(s_bad, 1)
            mm(bE[0:1, 0:1], bad_sum[:, 0:1], ones[0:G, 0:1], start=True, stop=True).then_inc(s_flag_ps, 1)
            pe.wait_ge(s_w, 160)
            nc.tensor.transpose(bM[:, 0:D], W2[:, :], ident[:, :]).then_inc(s_w2t_ps, 1)
            pe.wait_ge(s_w2t, 1)
            pe.wait_ge(s_flag, 1)
            mm(bE[:, 0:D], W2T[:, :], U1b[:, :], start=True, stop=True)
            mm(bE[:, D:D + 1], U1b[:, :], b2[:, 0:1], start=True, stop=True).then_inc(s_v_ps, 1)
            pe.wait_ge(s_idf, 3)
            for t, bank in ((sf, bT[0]), (df, bT[1]), (wf, bP[0])):
                for c in range(C):
                    last = nc.tensor.transpose(bank[:, c * G:(c + 1) * G],
                                               t[:, :].rearrange("g (p c) -> g c p", c=C)[:, c, :], ident[0:G, 0:G])
                last.then_inc(s_idx_ps, 1)
            pe.wait_ge(s_bad, 2)
            pe.wait_ge(s_v, 2)
            mm(bE[0:1, 256:257], bad_sum[:, 1:2], ones[0:G, 0:1], start=True, stop=True).then_inc(s_flag_ps, 1)

            def transpose4(bank, tiles, width=P):
                for k, t in enumerate(tiles):
                    last = nc.tensor.transpose(bank[0:width, k * P:(k + 1) * P], t, ident[:, :])
                return last

            def quarter(s, q):
                return [y[s][:, k, :] for k in range(4 * q, 4 * q + 4)]

            def update(g, k, h):
                pe.wait_ge(a_hT, Q * g + k + 1)
                mm(bP[PB[k]][:, :], U1a[:, :], h[:, :], start=True, stop=True).then_inc(p_pre, 1)

            def output(bank, u):
                for c in range(4):
                    last = mm(bank[:, c * D:(c + 1) * D], u[:, c, :], U2[:, :], start=True, stop=True)
                return last

            pe.wait_ge(s_idx, 3)
            pe.wait_ge(s_y, 1)
            transpose4(bT[0], quarter(0, 0)).then_inc(p_hT, 1)

            def group(g, s, n, more):
                pe.wait_ge(s_y, Q * g + 2)
                wait(pe, a_hT, Q * g)
                pe.wait_ge(s_ea[s], 32 * n)
                wait(pe, a_m, g)
                transpose4(bT[1], quarter(s, 1)).then_inc(p_hT, 1)
                transpose4(bM, [ea[s][:, c, :] for c in range(C)], DE).then_inc(p_ea, 1)
                pe.wait_ge(s_ye, 2 * g + 1)
                pe.wait_ge(a_hT, Q * g + 1)
                transpose4(bT[0], [ys[s][:, c, :] for c in range(C)]).then_inc(p_hs, 1)
                wait(pe, a_u, Q * g)
                update(g, 0, hT[0])
                pe.wait_ge(s_y, Q * g + 3)
                pe.wait_ge(a_hT, Q * g + 2)
                transpose4(bT[1], quarter(s, 2)).then_inc(p_hT, 1)
                pe.wait_ge(a_hs, g + 1)
                mm(bP[1][:, :], W1a[:, :], hsT[:, :], start=True, stop=False)
                pe.wait_ge(a_ea, g + 1)
                mm(bP[1][:, :], W1b[:, :], eaT[:, :], start=False, stop=True).then_inc(p_z, 1)
                pe.wait_ge(a_u, Q * g + 1)
                update(g, 1, hT[1])
                pe.wait_ge(s_ye, 2 * g + 2)
                transpose4(bT[0], [yd[s][:, c, :] for c in range(C)]).then_inc(p_hd, 1)
                pe.wait_ge(a_z, g + 1)
                mm(bM[:, :], V[:, :], zT[:, :], start=True, stop=True).then_inc(p_m, 1)
                wait(pe, v_out, Q * g)
                pe.wait_ge(a_u, Q * g + 1)
                output(bO[0], uT[0]).then_inc(p_out, 1)
                pe.wait_ge(a_hd, g + 1)
                mm(bP[1][:, :], U1a[:, :], hdT[:, :], start=True, stop=True).then_inc(p_pree, 1)
                pe.wait_ge(s_y, Q * g + 4)
                pe.wait_ge(a_hT, Q * g + 3)
                transpose4(bT[1], quarter(s, 3)).then_inc(p_hT, 1)
                pe.wait_ge(a_u, Q * g + 2)
                update(g, 2, hT[0])
                output(bO[1], uT[1]).then_inc(p_out, 1)
                pe.wait_ge(v_pree, g + 1)
                update(g, 3, hT[1])
                pe.wait_ge(a_u, Q * g + 3)
                pe.wait_ge(v_out, Q * g + 1)
                output(bO[0], uT[2]).then_inc(p_out, 1)
                if more:
                    pe.wait_ge(s_y, Q * g + 5)
                    transpose4(bT[0], quarter(1 - s, 0)).then_inc(p_hT, 1)
                pe.wait_ge(a_ue, g + 1)
                wait(pe, v_oute, g)
                output(bE, ueT).then_inc(p_oute, 1)
                pe.wait_ge(a_u, Q * g + 4)
                pe.wait_ge(v_out, Q * g + 2)
                output(bO[1], uT[3]).then_inc(p_out, 1)

            group(0, 0, 1, True)
            group(1, 1, 1, True)
            with pe.Fori(1, LAST // 2) as i:
                group(2 * i, 0, i + 1, True)
                group(2 * i + 1, 1, i + 1, True)
            group(LAST, 0, LAST // 2 + 1, False)


_INS = ['x', 'src', 'dst', 'edge_attr_64', 'L0_gnn_msg_w1', 'L0_gnn_msg_b1', 'L0_gnn_msg_w2', 'L0_gnn_msg_b2',
        'L0_gnn_upd_w1', 'L0_gnn_upd_b1', 'L0_gnn_upd_w2', 'L0_gnn_upd_b2']


def kernel(**inputs):
    import numpy as _np
    import concourse.bacc as _bacc
    from concourse import mybir as _mybir
    from concourse.bass_utils import run_bass_kernel_spmd as _run

    nc = _bacc.Bacc("TRN2", target_bir_lowering=False, num_devices=1)
    arrays, args = {}, []
    for name in _INS:
        a = _np.ascontiguousarray(inputs[name])
        arrays[f"in_{name}_dram"] = a
        args.append(nc.dram_tensor(f"in_{name}_dram", a.shape, _mybir.dt.from_np(a.dtype), kind="ExternalInput").ap())
    x = arrays["in_x_dram"]
    args.append(nc.dram_tensor("out_dram", x.shape, _mybir.dt.from_np(x.dtype), kind="ExternalOutput").ap())
    bass_preln_gnn(nc, *args)
    r = _run(nc, [arrays], core_ids=[0])
    return r.results[0]["out_dram"]
```

```python
import concourse.bass as bass
from concourse import mybir
from concourse.alu_op_type import AluOpType as ALU
from contextlib import ExitStack


def bass_preln_gnn(
    nc: bass.Bass,
    x: bass.AP,
    src: bass.AP,
    dst: bass.AP,
    edge_attr: bass.AP,
    msg_w1: bass.AP,
    msg_b1: bass.AP,
    msg_w2: bass.AP,
    msg_b2: bass.AP,
    upd_w1: bass.AP,
    upd_b1: bass.AP,
    upd_w2: bass.AP,
    upd_b2: bass.AP,
    out: bass.AP,
):
    f32 = mybir.dt.float32
    bf16 = mybir.dt.bfloat16
    i32 = mybir.dt.int32
    ACT = mybir.ActivationFunctionType
    AX = mybir.AxisListType

    NODES, D = x.shape
    EDGES, DE = edge_attr.shape
    EPS = 1e-5
    P = 128
    T = 16
    GN = P * T
    C = 4
    GE = P * C
    Q = T // 4
    G = -(-NODES // GN)
    LAST = G - 1
    R = 4
    assert 2 * DE == P and C == 4
    assert G == -(-EDGES // GE) and LAST % R == 0
    NODE_LAST = NODES - GN
    EDGE_LAST = EDGES - GE
    CARRY_LAST = EDGE_LAST - 1 - (LAST - 1) * GE
    FAR = 1 << 20
    SQD = float(D) ** 0.5
    NT = T + 2 * C

    LN = 12
    SB = 10
    SW = EDGES // SB
    FLAT = 4 * SW + (4 + SB) * GE + 2
    assert SW * SB == EDGES

    ctx = ExitStack()
    with ctx:
        def sb(name, shape, dt=f32):
            return ctx.enter_context(nc.sbuf_tensor(name, shape, dt))

        def ps(name):
            return ctx.enter_context(nc.psum_tensor(name, [P, 512], f32))

        def sem(name):
            return ctx.enter_context(nc.semaphore(name))

        mask_dram = nc.dram_tensor("mask_dram", [G, GE], bf16, kind="Internal").ap()
        src_sorted = nc.dram_tensor("src_sorted", [EDGES, 1], i32, kind="Internal").ap()
        dst_sorted = nc.dram_tensor("dst_sorted", [EDGES, 1], i32, kind="Internal").ap()
        erow_dram = nc.dram_tensor("erow_dram", [G * GE, D], f32, kind="Internal").ap()
        attr_sorted = nc.dram_tensor("attr_sorted", [EDGES, DE], f32, kind="Internal").ap()

        W1a, W1b = sb("W1a", [D, D]), sb("W1b", [DE, D])
        W2, W2T, U1b, V = sb("W2", [D, D]), sb("W2T", [D, D]), sb("U1b", [D, D]), sb("V", [D, D])
        U1a, U2 = sb("U1a", [D, D]), sb("U2", [D, D])
        b1, b2, c1, vb = sb("b1", [D, 1]), sb("b2", [D, 1]), sb("c1", [D, 1]), sb("vb", [D, 1])
        c2 = sb("c2", [3, D])
        c2_hi, c2_mid, c2_lo = (sb(n, [3, D], bf16) for n in ("c2_hi", "c2_mid", "c2_lo"))
        c2_rest, c2_rest2, c2_sum, c2_sum2 = (sb(n, [3, D]) for n in ("c2_rest", "c2_rest2", "c2_sum", "c2_sum2"))
        c2_parts = sb("c2_parts", [3, 4, D], bf16)
        ones3 = sb("ones3", [3, P], bf16)
        ident = sb("ident", [P, P])
        ones = sb("ones", [P, 1])
        pad = sb("pad", [1, 2])

        xin = [sb(f"xin{s}", [P, T, D]) for s in range(R)]
        y = [sb(f"y{s}", [P, T, D]) for s in range(2)]
        hT = [sb(f"hT{s}", [D, 512]) for s in range(2)]
        uT = [sb(f"uT{q}", [D, 4, P]) for q in range(Q)]

        xs = [sb(f"xs{s}", [P, C, D]) for s in range(2)]
        xd = [sb(f"xd{s}", [P, C, D]) for s in range(R)]
        ys = [sb(f"ys{s}", [P, C, D]) for s in range(2)]
        yd = [sb(f"yd{s}", [P, C, D]) for s in range(2)]
        ea = [sb(f"ea{s}", [P, C, DE]) for s in range(2)]
        mask = [sb(f"mask{s}", [P, GE], bf16) for s in range(2)]
        run = [sb(f"run{s}", [D, GE]) for s in range(2)]
        hsT, hdT, eaT = sb("hsT", [D, GE]), sb("hdT", [D, GE]), sb("eaT", [DE, GE])
        zT, mT, preT, ueT = sb("zT", [D, GE]), sb("mT", [D, GE]), sb("preT", [D, GE]), sb("ueT", [D, C, P])
        flat = sb("flat", [G, FLAT])

        st = sb("st", [P, NT, 6])
        st_sum, st_dif = sb("st_sum", [P, NT]), sb("st_dif", [P, NT])
        st_q, st_dd, st_v = sb("st_q", [P, NT]), sb("st_dd", [P, NT]), sb("st_v", [P, NT])
        st_root, st_r = sb("st_root", [P, NT]), sb("st_r", [P, NT])
        mean = [sb(f"mean{s}", [P, NT]) for s in range(2)]
        rstd = [sb(f"rstd{s}", [P, NT]) for s in range(2)]
        shift = [sb(f"shift{s}", [P, NT]) for s in range(2)]

        DEXT = FLAT - GE - 2
        dext = flat[0:G, DEXT:DEXT + GE + 2].bitcast(i32)
        d_prev, d_cur, d_next = dext[:, 0:GE], dext[:, 1:GE + 1], dext[:, 2:GE + 2]
        srow = ueT[0:G, :, :].rearrange("g c p -> g (c p)").bitcast(i32)
        gidx = sb("gidx", [G, 1], i32)
        bound = sb("bound", [G, 1])
        lastg = sb("lastg", [G, 1])
        far_flag = sb("far_flag", [G, 1])
        sf, df, wf = hsT[0:G, :], hdT[0:G, :], zT[0:G, :]
        same_next, bad = mT[0:G, :], preT[0:G, :]
        bad_sum = sb("bad_sum", [G, 2])
        mrow = sb("mrow", [G, GE], bf16)
        src_idx, dst_idx, out_idx = (sb(n, [P, G, C], i32) for n in ("src_idx", "dst_idx", "out_idx"))
        g_idx = [sb(f"g_idx{s}", [P, 2, C], i32) for s in range(R)]
        o_idx = [sb(f"o_idx{s}", [P, C], i32) for s in range(R)]
        rank_col, src_col, dst_col = (o_idx[0][0:G, n:n + 1] for n in range(3))
        flags = sb("flags", [1, 2], i32)

        bT = [ps("bT0"), ps("bT1")]
        bP = [ps("bP0"), ps("bP1")]
        bO = [ps("bO0"), ps("bO1")]
        bM, bE = ps("bM"), ps("bE")

        s_x = [sem(f"s_x{s}") for s in range(R)]
        s_ea = [sem(f"s_ea{s}") for s in range(2)]
        s_src = [sem(f"s_src{s}") for s in range(2)]
        s_store = [sem(f"s_store{s}") for s in range(R)]
        s_erow = [sem(f"s_erow{s}") for s in range(R)]
        s_scat, s_back = sem("s_scat"), sem("s_back")
        s_w, s_dext, s_srow, s_mstore = sem("s_w"), sem("s_dext"), sem("s_srow"), sem("s_mstore")
        s_fill, s_ident, s_iota = sem("s_fill"), sem("s_ident"), sem("s_iota")
        s_idc, s_bad = sem("s_idc"), sem("s_bad")
        s_sorted_keys = sem("s_sorted_keys")
        s_flag_ps, s_flag = sem("s_flag_ps"), sem("s_flag")
        s_mrow, s_idf, s_idx_ps, s_idx = sem("s_mrow"), sem("s_idf"), sem("s_idx_ps"), sem("s_idx")
        s_w2t_ps, s_w2t, s_v_ps, s_v = sem("s_w2t_ps"), sem("s_w2t"), sem("s_v_ps"), sem("s_v")
        s_ln = sem("s_ln")
        s_root = sem("s_root")
        s_tiles_stats = sem("s_tiles_stats")
        s_y = sem("s_y")
        s_ye = sem("s_ye")
        s_c2 = sem("s_c2")
        p_hT, p_ea, p_hs, p_hd = sem("p_hT"), sem("p_ea"), sem("p_hs"), sem("p_hd")
        p_pre, p_z, p_m, p_pree, p_out, p_oute = (sem(n) for n in ("p_pre", "p_z", "p_m", "p_pree", "p_out", "p_oute"))
        a_hT, a_ea, a_hs, a_hd, a_u, a_z, a_m, a_ue = (sem(n) for n in ("a_hT", "a_ea", "a_hs", "a_hd", "a_u", "a_z", "a_m", "a_ue"))
        v_run, v_pree, v_out, v_oute = sem("v_run"), sem("v_pree"), sem("v_out"), sem("v_oute")
        v_init = sem("v_init")
        r_blk, r_step, r_rank, r_row, r_scat, r_dma = (sem(n) for n in ("r_blk", "r_step", "r_rank", "r_row", "r_scat", "r_dma"))
        r_iota, r_col = sem("r_iota"), sem("r_col")
        s_gi, s_oi = sem("s_gi"), sem("s_oi")

        dst_blk = flat[0:G, 0:SW].bitcast(i32)
        pos_blk = flat[0:G, SW:2 * SW]
        cmp_a, cmp_b = flat[0:G, 2 * SW:3 * SW], flat[0:G, 3 * SW:4 * SW]
        base_f = 4 * SW
        own = flat[0:G, base_f:base_f + GE]
        own_b = flat[0:G, base_f + GE:base_f + 2 * GE]
        part = flat[0:G, base_f + 2 * GE:base_f + 2 * GE + SB * GE].rearrange("p (b c) -> p b c", b=SB)
        rank = flat[0:G, base_f + (2 + SB) * GE:base_f + (3 + SB) * GE].bitcast(i32)
        attr_row = cmp_a[:, 0:DE]

        def wait(eng, s, count):
            if not (isinstance(count, int) and count <= 0):
                eng.wait_ge(s, count)

        def filled(i, k, slots):
            return (R // slots) * i + k // slots + 1

        def node_rows(t, base):
            return t[bass.ds(base, GN), :].rearrange("(p t) d -> p t d", t=T)

        def attr_rows(t, base):
            return t[bass.ds(base, GE), :].rearrange("(p c) d -> p c d", c=C)

        def col(v):
            return v.rearrange("(n a) -> n a", a=1)

        block = ctx.enter_context(nc.Block())

        @block.sync
        def _(sp):
            def load_x(base, s):
                sp.dma_start(xin[s][:, :, :], node_rows(x, base)).then_inc(s_x[s], 16)

            def load_keys(d):
                mid = bass.AP(tensor=d.tensor, offset=d.offset + GE - 1, ap=[[GE, LAST - 1], [1, GE + 2]])
                sp.dma_start(dext[1:LAST, :], mid).then_inc(s_dext, 16)
                sp.dma_start(dext[0:1, 1:GE + 2], d[0:GE + 1].rearrange("(a n) -> a n", a=1)).then_inc(s_dext, 16)
                sp.dma_start(dext[LAST:G, 0:GE + 1], d[EDGE_LAST - 1:EDGES].rearrange("(a n) -> a n", a=1)).then_inc(s_dext, 16)

            def load_src(v):
                sp.dma_start(srow[0:LAST, :], v[0:LAST * GE].rearrange("(g n) -> g n", n=GE)).then_inc(s_srow, 16)
                sp.dma_start(srow[LAST:G, :], v[EDGE_LAST:EDGES].rearrange("(g n) -> g n", n=GE)).then_inc(s_srow, 16)

            sp.wait_ge(s_fill, 2)
            load_keys(dst)
            load_x(0, 0)
            load_src(src)
            for t, v in ((W1a, msg_w1[0:D, :]), (W1b, msg_w1[D:D + DE, :]), (W2, msg_w2), (U1a, upd_w1[0:D, :]),
                         (U1b, upd_w1[D:2 * D, :]), (U2, upd_w2), (b1, col(msg_b1)), (b2, col(msg_b2)),
                         (c1, col(upd_b1)), (c2, upd_b2.partition_broadcast(3))):
                sp.dma_start(t[:, :], v).then_inc(s_w, 16)
            load_x(GN, 1)
            load_x(2 * GN, 2)

            sp.wait_ge(s_flag, 1)
            unsorted = sp.value_load(flags[0:1, 0:1])
            with sp.If(unsorted != 0):
                for b in range(SB):
                    if b:
                        sp.wait_ge(r_step, 4 * GE * b)
                    sp.dma_start(dst_blk, dst[b * SW:(b + 1) * SW].partition_broadcast(G)).then_inc(r_blk, 16)
                sp.wait_ge(r_rank, 1)

                def attr_column(c):
                    rest = edge_attr[0:LAST * GE, :].rearrange("(g n) d -> g n d", n=GE)[:, c, :]
                    sp.dma_start(attr_row[0:LAST, :], rest).then_inc(r_row, 16)
                    sp.dma_start(attr_row[LAST:G, :], edge_attr[bass.ds(c + EDGE_LAST, 1), :]).then_inc(r_row, 16)

                attr_column(0)
                with sp.Fori(1, GE) as c:
                    sp.wait_ge(r_scat, c * 48)
                    attr_column(c)
                sp.wait_ge(r_scat, GE * 48)
                load_keys(dst_sorted.rearrange("n a -> (n a)"))
                load_src(src_sorted.rearrange("n a -> (n a)"))
                sp.wait_ge(s_dext, 96)
                sp.wait_ge(s_srow, 64)
            sp.wait_ge(s_dext, 48)
            sp.wait_ge(s_srow, 32)
            sp.sem_inc(s_sorted_keys, 1)

            sp.wait_ge(s_mrow, 1)
            sp.dma_start(mask_dram, mrow[:, :]).then_inc(s_mstore, 16)
            sp.wait_ge(s_mstore, 16)

            def load_edges(g, base, s):
                m = mask_dram[bass.ds(g, 1), :].rearrange("a n -> (a n)")
                sp.dma_start(mask[s][:, :], m.partition_broadcast(P)).then_inc(s_ea[s], 16)
                with sp.If(unsorted != 0):
                    sp.dma_start(ea[s][:, :, :], attr_rows(attr_sorted, base)).then_inc(s_ea[s], 16)
                with sp.If(unsorted == 0):
                    sp.dma_start(ea[s][:, :, :], attr_rows(edge_attr, base)).then_inc(s_ea[s], 16)

            load_edges(0, 0, 0)
            load_edges(1, GE, 1)

            def step(i, k):
                g = R * i + k
                static = isinstance(g, int)
                if not static or g + 3 <= LAST:
                    if not static or g > 0:
                        sp.wait_ge(s_store[(k - 1) % R], 16 * filled(i, k - 1, R))
                    load_x(NODE_LAST if static and g + 3 == LAST else (g + 3) * GN, (k + 3) % R)
                if not static or g + 2 <= LAST:
                    sp.wait_ge(p_ea, g + 1)
                    sp.wait_ge(v_run, g + 1)
                    load_edges(g + 2, EDGE_LAST if static and g + 2 == LAST else (g + 2) * GE, k % 2)
                sp.wait_ge(v_out, Q * (g + 1))
                if static and g == LAST:
                    sp.wait_ge(s_store[(k - 1) % R], 16 * filled(i, k - 1, R))
                sp.dma_start(node_rows(out, NODE_LAST if static and g == LAST else g * GN),
                             xin[k % R][:, :, :]).then_inc(s_store[k % R], 16)

            for k in range(R):
                step(0, k)
            with sp.Fori(1, LAST // R - 1) as i:
                for k in range(R):
                    step(i, k)
            for k in range(R):
                step(LAST // R - 1, k)
            step(LAST // R, 0)
            for k in range(R):
                sp.wait_ge(s_store[k], 16 * (LAST // R + (k == 0)))

        @block.gpsimd
        def _(pool):
            def carry_wait(n=0):
                pool.tensor_tensor(out=pad[:, n:n + 1], in0=ident[0:1, 0:1], in1=ident[0:1, 0:1], op=ALU.add)

            pool.memset(dext[:, 0:1], -1).then_inc(s_fill, 1)
            pool.memset(dext[:, GE + 1:GE + 2], FAR).then_inc(s_fill, 1)
            pool.iota(gidx[:, :], pattern=[[0, 1]], base=0, channel_multiplier=1).then_inc(s_iota, 1)
            pool.memset(ident[:, :], 0.0).then_inc(s_ident, 1)
            pool.memset(ones[:, :], 1.0).then_inc(s_ident, 1)
            pool.wait_ge(s_ident, 2)
            pool.affine_select(out=ident[:, :], in_=ident[:, :], compare_op=ALU.not_equal, fill=1.0,
                               base=0, pattern=[[-1, P]], channel_multiplier=1).then_inc(s_ident, 1)
            pool.wait_ge(s_ident, 3)

            pool.wait_ge(s_flag, 1)
            unsorted = pool.value_load(flags[0:1, 0:1])
            with pool.If(unsorted != 0):
                pool.iota(pos_blk, pattern=[[1, SW]], base=0, channel_multiplier=0,
                          allow_small_or_imprecise_dtypes=True).then_inc(r_iota, 1)
                pool.iota(own, pattern=[[1, GE]], base=0, channel_multiplier=0,
                          allow_small_or_imprecise_dtypes=True).then_inc(r_iota, 1)
                pool.wait_ge(r_rank, 1)
                pool.wait_ge(s_srow, 32)
                with pool.Fori(0, GE) as c:
                    pool.wait_ge(r_row, (c + 1) * 32)
                    pool.tensor_copy(rank_col, rank[:, bass.ds(c, 1)]).then_inc(r_col, 1)
                    pool.tensor_copy(src_col, srow[:, bass.ds(c, 1)]).then_inc(r_col, 1)
                    pool.tensor_copy(dst_col, dext[:, bass.ds(c + 1, 1)]).then_inc(r_col, 1)
                    pool.wait_ge(r_col, 3 * (c + 1))
                    carry_wait()
                    off = bass.IndirectOffsetOnAxis(rank_col, 0)
                    pool.indirect_dma_start(attr_sorted, off, attr_row, None).then_inc(r_scat, 16)
                    pool.indirect_dma_start(src_sorted, off, src_col, None).then_inc(r_scat, 16)
                    pool.indirect_dma_start(dst_sorted, off, dst_col, None).then_inc(r_scat, 16)
                    pool.wait_ge(r_scat, (c + 1) * 48)
                    carry_wait(1)
            pool.wait_ge(s_flag, 2)
            late = pool.value_load(flags[0:1, 1:2])
            pool.wait_ge(s_idx, 3)

            def indices(g, r):
                pool.tensor_copy(g_idx[r][:, 0, :], src_idx[:, g, :]).then_inc(s_gi, 1)
                pool.tensor_copy(g_idx[r][:, 1, :], dst_idx[:, g, :]).then_inc(s_gi, 1)

            def gather(s, r):
                for n, t in enumerate((xs[s], xd[r])):
                    for c in range(C):
                        pool.indirect_dma_start(t[:, c, :], None, x,
                                                bass.IndirectOffsetOnAxis(g_idx[r][:, n, c:c + 1], 0)).then_inc(s_src[s], 16)

            def row_indices(g, s):
                pool.tensor_copy(o_idx[s][:, :], out_idx[:, g, :]).then_inc(s_oi, 1)
                pool.wait_ge(s_oi, g + 1)
                carry_wait()

            def scatter(s, done):
                for c in range(C):
                    pool.indirect_dma_start(out, bass.IndirectOffsetOnAxis(o_idx[s][:, c:c + 1], 0),
                                            xd[s][:, c, :], None,
                                            bounds_check=NODES - 1, oob_is_err=False).then_inc(done, 16)

            indices(0, 0)
            indices(1, 1)
            pool.wait_ge(s_gi, 4)
            gather(0, 0)
            gather(1, 1)

            def step(i, k):
                g = R * i + k
                static = isinstance(g, int)
                if not static or g + 2 <= LAST:
                    indices(g + 2, (k + 2) % R)
                    pool.wait_ge(s_gi, 2 * g + 6)
                    pool.wait_ge(s_ye, 2 * (g + 1))
                    if not static or g >= 2:
                        pool.wait_ge(s_erow[(k - 2) % R], C * 16 * filled(i, k - 2, R))
                    carry_wait()
                    gather(k % 2, (k + 2) % R)
                if not static or g > 0:
                    p = (k - 1) % R
                    pool.wait_ge(v_oute, g)
                    pool.wait_ge(s_store[p], 16 * filled(i, k - 1, R))
                    row_indices(g - 1, p)
                    with pool.If(late == 0):
                        scatter(p, s_erow[p])
                    with pool.If(late != 0):
                        for c in range(C):
                            pool.dma_start(erow_dram[bass.ds((g - 1) * GE + c * P, P), :],
                                           xd[p][:, c, :]).then_inc(s_erow[p], 16)

            for k in range(R):
                step(0, k)
            with pool.Fori(1, LAST // R - 1) as i:
                for k in range(R):
                    step(i, k)
            for k in range(R):
                step(LAST // R - 1, k)
            step(LAST // R, 0)
            pool.wait_ge(v_oute, G)
            row_indices(LAST, 0)
            pool.wait_ge(s_store[0], 16 * (LAST // R + 1))
            for k in range(R):
                pool.wait_ge(s_erow[k], C * 16 * (LAST // R))
            scatter(0, s_scat)
            pool.wait_ge(s_scat, 16 * C)
            with pool.If(late != 0):
                with pool.Fori(0, LAST) as g:
                    pool.tensor_copy(o_idx[0][:, :], out_idx[:, g, :]).then_inc(s_oi, 1)
                    for c in range(C):
                        pool.dma_start(xd[0][:, c, :], erow_dram[bass.ds(g * GE + c * P, P), :]).then_inc(s_back, 16)
                    pool.wait_ge(s_back, 16 * C * (g + 1))
                    pool.wait_ge(s_oi, G + g + 1)
                    carry_wait()
                    scatter(0, s_scat)
                    pool.wait_ge(s_scat, 16 * C * (g + 2))
                    carry_wait(1)

        @block.scalar
        def _(act):
            def relu_scaled(o, i):
                return nc.scalar.activation(o, i, ACT.Relu, scale=SQD)

            def norm_edges(s, r, js):
                for j in js:
                    t, tile, k = (xs[s], ys, j) if j < C else (xd[r], yd, j - C)
                    last = nc.scalar.activation(tile[s][:, k, :], t[:, k, :], ACT.Identity,
                                                scale=rstd[s][:, T + j:T + j + 1], bias=shift[s][:, T + j:T + j + 1])
                    if k == C - 1:
                        last.then_inc(s_ye, 1)

            act.wait_ge(s_w2t_ps, 1)
            nc.scalar.activation(W2T[:, :], bM[:, 0:D], ACT.Copy).then_inc(s_w2t, 1)
            act.wait_ge(s_v_ps, 1)
            nc.scalar.activation(V[:, :], bE[:, 0:D], ACT.Copy).then_inc(s_v, 1)
            nc.scalar.activation(vb[:, :], bE[:, D:D + 1], ACT.Copy).then_inc(s_v, 1)
            act.wait_ge(s_v, 2)
            act.wait_ge(s_w, 160)

            def root(g):
                act.wait_ge(s_ln, LN * g + 7)
                nc.scalar.activation(st_root[:, :], st_v[:, :], ACT.Sqrt).then_inc(s_root, 1)

            root(0)
            act.wait_ge(p_hT, 1)
            relu_scaled(hT[0][:, :], bT[0][:, :]).then_inc(a_hT, 1)
            act.wait_ge(s_ln, LN)
            norm_edges(0, 0, range(2 * C))

            def evac_u(g, k):
                act.wait_ge(p_pre, Q * g + k + 1)
                nc.scalar.activation(uT[k][:, :, :].rearrange("d c p -> d (c p)"), bP[0][:, :], ACT.Relu,
                                     bias=c1[:, 0:1]).then_inc(a_u, 1)

            def group(i, k):
                g, s = R * i + k, k % 2
                more = not isinstance(g, int) or g < LAST
                act.wait_ge(p_hT, Q * g + 2)
                relu_scaled(hT[1][:, :], bT[1][:, :]).then_inc(a_hT, 1)
                act.wait_ge(p_ea, g + 1)
                for h in range(2):
                    last = nc.scalar.activation(eaT[:, :].rearrange("d (j h p) -> d h j p", j=2, h=2)[:, h, :, :],
                                                bM[h * DE:(h + 1) * DE, 0:2 * P].rearrange("d (j p) -> d j p", j=2), ACT.Copy)
                last.then_inc(a_ea, 1)
                act.wait_ge(p_hs, g + 1)
                relu_scaled(hsT[:, :], bT[0][:, :]).then_inc(a_hs, 1)
                evac_u(g, 0)
                act.wait_ge(p_hT, Q * g + 3)
                relu_scaled(hT[0][:, :], bT[1][:, :]).then_inc(a_hT, 1)
                act.wait_ge(p_z, g + 1)
                nc.scalar.activation(zT[:, :], bP[1][:, :], ACT.Relu, bias=b1[:, 0:1]).then_inc(a_z, 1)
                evac_u(g, 1)
                act.wait_ge(p_hd, g + 1)
                relu_scaled(hdT[:, :], bT[0][:, :]).then_inc(a_hd, 1)
                act.wait_ge(p_m, g + 1)
                wait(act, v_run, g)
                nc.scalar.activation(mT[:, :].rearrange("d (p c) -> d c p", c=C),
                                     bM[:, :].rearrange("d (c p) -> d c p", c=C), ACT.Identity,
                                     bias=vb[:, 0:1]).then_inc(a_m, 1)
                if more:
                    root(g + 1)
                act.wait_ge(p_hT, Q * g + 4)
                relu_scaled(hT[1][:, :], bT[1][:, :]).then_inc(a_hT, 1)
                evac_u(g, 2)
                act.wait_ge(v_pree, g + 1)
                nc.scalar.activation(ueT[:, :, :].rearrange("d c p -> d (c p)"), preT[:, :], ACT.Relu,
                                     bias=c1[:, 0:1]).then_inc(a_ue, 1)
                if more:
                    act.wait_ge(s_ln, LN * (g + 2))
                    norm_edges(1 - s, (k + 1) % R, range(0, 4))
                evac_u(g, 3)
                if more:
                    norm_edges(1 - s, (k + 1) % R, range(4, 8))
                    act.wait_ge(p_hT, Q * g + 5)
                    relu_scaled(hT[0][:, :], bT[0][:, :]).then_inc(a_hT, 1)

            for k in range(R):
                group(0, k)
            with act.Fori(1, LAST // R) as i:
                for k in range(R):
                    group(i, k)
            group(LAST // R, 0)

        @block.vector
        def _(dve):
            nc.vector.memset(run[1][:, :], 0.0).then_inc(v_init, 1)
            nc.vector.memset(ones3[:, :], 1.0).then_inc(v_init, 1)

            def stats(r, js):
                for j in js:
                    t, k = (xin[r], j) if j < T else (xs[r % 2], j - T) if j < T + C else (xd[r], j - T - C)
                    last = nc.vector.bn_stats(st[:, j, :], t[:, k, :])
                return last

            dve.wait_ge(s_dext, 48)
            dve.wait_ge(s_fill, 2)
            nc.vector.tensor_tensor(out=bad[:, :], in0=d_cur, in1=d_next, op=ALU.is_gt).then_inc(s_idc, 1)
            dve.wait_ge(s_idc, 1)
            nc.vector.reduce_sum(bad_sum[:, 0:1], bad[:, :], axis=AX.X).then_inc(s_bad, 1)
            dve.wait_ge(s_flag_ps, 1)
            nc.vector.tensor_copy(flags[0:1, 0:1], bE[0:1, 0:1]).then_inc(s_flag, 1)

            dve.wait_ge(s_flag, 1)
            unsorted = dve.value_load(flags[0:1, 0:1])
            with dve.If(unsorted != 0):
                dve.wait_ge(r_iota, 2)
                dve.wait_ge(s_iota, 1)
                nc.vector.tensor_copy(df[:, :], d_cur).then_inc(r_dma, 1)
                nc.vector.tensor_scalar(bound[:, :], gidx[:, :], float(GE), float(EDGE_LAST), ALU.mult, ALU.min).then_inc(r_dma, 1)
                dve.wait_ge(r_dma, 2)
                nc.vector.tensor_scalar(own, own, bound[:, 0:1], None, ALU.add).then_inc(r_dma, 1)
                dve.wait_ge(r_dma, 3)
                for b in range(SB):
                    dve.wait_ge(r_blk, 16 * (b + 1))
                    nc.vector.tensor_scalar(own_b, own, float(b * SW), None, ALU.subtract).then_inc(r_dma, 1)
                    dve.wait_ge(r_dma, b + 4)
                    def count_column(c):
                        n = c * 4 + b * 4 * GE
                        wait(dve, r_step, n)
                        nc.vector.tensor_scalar(cmp_a, dst_blk, df[:, bass.ds(c, 1)], 32768.0, ALU.subtract, ALU.mult).then_inc(r_step, 1)
                        dve.wait_ge(r_step, n + 1)
                        nc.vector.scalar_tensor_tensor(out=cmp_b, in0=cmp_a, scalar=own_b[:, bass.ds(c, 1)], in1=pos_blk,
                                                       op0=ALU.subtract, op1=ALU.add).then_inc(r_step, 1)
                        dve.wait_ge(r_step, n + 2)
                        nc.vector.tensor_scalar(cmp_a, cmp_b, 0.0, None, ALU.is_lt).then_inc(r_step, 1)
                        dve.wait_ge(r_step, n + 3)
                        nc.vector.reduce_sum(part[:, b, bass.ds(c, 1)], cmp_a, axis=AX.X).then_inc(r_step, 1)

                    count_column(0)
                    with dve.Fori(1, GE) as c:
                        count_column(c)
                    dve.wait_ge(r_step, (b + 1) * 4 * GE)
                nc.vector.reduce_sum(own_b, part.rearrange("p b c -> p c b"), axis=AX.X).then_inc(r_dma, 1)
                dve.wait_ge(r_dma, SB + 4)
                nc.vector.tensor_copy(rank, own_b).then_inc(r_rank, 1)

            dve.wait_ge(s_sorted_keys, 1)
            dve.wait_ge(s_iota, 1)
            V_ = nc.vector
            V_.tensor_tensor(out=mrow[:, :], in0=d_cur, in1=d_prev, op=ALU.is_equal).then_inc(s_mrow, 1)
            V_.tensor_tensor(out=same_next[:, :], in0=d_cur, in1=d_next, op=ALU.is_equal).then_inc(s_idc, 1)
            V_.tensor_copy(df[:, :], d_cur).then_inc(s_idf, 1)
            V_.tensor_copy(sf[:, :], srow[:, :]).then_inc(s_idf, 1)
            V_.tensor_scalar(bound[:, :], gidx[:, :], float(GN), float(GN), ALU.mult, ALU.add).then_inc(s_idc, 1)
            V_.tensor_scalar(lastg[:, :], gidx[:, :], float(LAST), float(FAR), ALU.is_equal, ALU.mult).then_inc(s_idc, 1)
            dve.wait_ge(s_idc, 4)
            V_.tensor_scalar(bound[:, :], bound[:, :], float(NODE_LAST), lastg[:, 0:1], ALU.min, ALU.add).then_inc(s_idc, 1)
            dve.wait_ge(s_idf, 2)
            V_.scalar_tensor_tensor(out=wf[:, :], in0=same_next[:, :], scalar=float(FAR), in1=df[:, :],
                                    op0=ALU.mult, op1=ALU.add).then_inc(s_idf, 1)
            dve.wait_ge(s_idc, 5)
            V_.tensor_scalar(bad[:, :], df[:, :], bound[:, 0:1], None, ALU.is_ge).then_inc(s_idc, 1)
            dve.wait_ge(s_idc, 6)
            V_.reduce_sum(bad_sum[:, 1:2], bad[:, :], axis=AX.X).then_inc(s_bad, 1)
            for n, (t, bank) in enumerate(((src_idx, bT[0]), (dst_idx, bT[1]), (out_idx, bP[0]))):
                dve.wait_ge(s_idx_ps, n + 1)
                V_.tensor_copy(t[:, :, :].rearrange("p g c -> p c g"),
                               bank[:, 0:C * G].rearrange("p (c g) -> p c g", c=C)).then_inc(s_idx, 1)
            dve.wait_ge(s_flag_ps, 2)
            V_.tensor_copy(flags[0:1, 1:2], bE[0:1, 256:257]).then_inc(s_flag, 1)

            def ln_variance(g, s):
                n = LN * g
                dve.wait_ge(s_tiles_stats, 2 * (g + 1))
                V_.tensor_tensor(out=st_dif[:, :], in0=st[:, :, 1], in1=st[:, :, 4], op=ALU.subtract).then_inc(s_ln, 1)
                V_.tensor_tensor(out=st_q[:, :], in0=st[:, :, 2], in1=st[:, :, 5], op=ALU.add).then_inc(s_ln, 1)
                V_.tensor_tensor(out=st_sum[:, :], in0=st[:, :, 1], in1=st[:, :, 4], op=ALU.add).then_inc(s_ln, 1)
                dve.wait_ge(s_ln, n + 1)
                V_.tensor_tensor(out=st_dd[:, :], in0=st_dif[:, :], in1=st_dif[:, :], op=ALU.mult).then_inc(s_ln, 1)
                dve.wait_ge(s_ln, n + 3)
                V_.tensor_scalar(mean[s][:, :], st_sum[:, :], 0.5, None, ALU.mult).then_inc(s_ln, 1)
                dve.wait_ge(s_ln, n + 4)
                V_.scalar_tensor_tensor(out=st_v[:, :], in0=st_dd[:, :], scalar=float(D) / 4, in1=st_q[:, :],
                                        op0=ALU.mult, op1=ALU.add).then_inc(s_ln, 1)
                dve.wait_ge(s_ln, n + 6)
                V_.tensor_scalar(st_v[:, :], st_v[:, :], float(D) * EPS, None, ALU.add).then_inc(s_ln, 1)

            def ln_rstd(g, s):
                n = LN * g + 7
                dve.wait_ge(s_root, g + 1)
                V_.reciprocal(st_r[:, :], st_root[:, :]).then_inc(s_ln, 1)
                dve.wait_ge(s_ln, n + 1)
                V_.scalar_tensor_tensor(out=st_dd[:, :], in0=st_r[:, :], scalar=-0.5, in1=st_r[:, :],
                                        op0=ALU.mult, op1=ALU.mult).then_inc(s_ln, 1)
                dve.wait_ge(s_ln, n + 2)
                V_.tensor_tensor(out=st_q[:, :], in0=st_dd[:, :], in1=st_v[:, :], op=ALU.mult).then_inc(s_ln, 1)
                dve.wait_ge(s_ln, n + 3)
                V_.scalar_tensor_tensor(out=rstd[s][:, :], in0=st_q[:, :], scalar=1.5, in1=st_r[:, :],
                                        op0=ALU.add, op1=ALU.mult).then_inc(s_ln, 1)
                dve.wait_ge(s_ln, n + 4)
                V_.scalar_tensor_tensor(out=shift[s][:, :], in0=mean[s][:, :], scalar=-1.0, in1=rstd[s][:, :],
                                        op0=ALU.mult, op1=ALU.mult).then_inc(s_ln, 1)

            def norm(g, r, q):
                s = r % 2
                dve.wait_ge(s_ln, LN * (g + 1) - 1)
                for k in range(4 * q, 4 * q + 4):
                    last = V_.tensor_scalar(y[s][:, k, :], xin[r][:, k, :], mean[s][:, k:k + 1], rstd[s][:, k:k + 1],
                                            ALU.subtract, ALU.mult)
                last.then_inc(s_y, 1)

            dve.wait_ge(s_w, 160)
            dve.wait_ge(s_ident, 2)
            V_.tensor_copy(c2_hi[:, :], c2[:, :]).then_inc(s_c2, 1)
            dve.wait_ge(s_c2, 1)
            V_.tensor_tensor(out=c2_rest[:, :], in0=c2[:, :], in1=c2_hi[:, :], op=ALU.subtract).then_inc(s_c2, 1)
            dve.wait_ge(s_c2, 2)
            V_.tensor_copy(c2_mid[:, :], c2_rest[:, :]).then_inc(s_c2, 1)
            dve.wait_ge(s_c2, 3)
            V_.tensor_tensor(out=c2_rest2[:, :], in0=c2_rest[:, :], in1=c2_mid[:, :], op=ALU.subtract).then_inc(s_c2, 1)
            dve.wait_ge(s_c2, 4)
            V_.tensor_copy(c2_lo[:, :], c2_rest2[:, :]).then_inc(s_c2, 1)
            dve.wait_ge(s_ident, 3)
            V_.tensor_scalar(c2_sum[:, :], c2_hi[:, :], ident[0:3, 0:1], None, ALU.mult).then_inc(s_c2, 1)
            dve.wait_ge(s_c2, 6)
            V_.scalar_tensor_tensor(out=c2_sum2[:, :], in0=c2_mid[:, :], scalar=ident[0:3, 1:2], in1=c2_sum[:, :],
                                    op0=ALU.mult, op1=ALU.add).then_inc(s_c2, 1)
            dve.wait_ge(s_c2, 7)
            for n in range(4):
                last = V_.scalar_tensor_tensor(out=c2_parts[:, n, :], in0=c2_lo[:, :], scalar=ident[0:3, 2:3],
                                               in1=c2_sum2[:, :], op0=ALU.mult, op1=ALU.add)
            last.then_inc(s_c2, 1)

            dve.wait_ge(s_x[0], 16)
            stats(0, range(T)).then_inc(s_tiles_stats, 1)
            dve.wait_ge(s_src[0], 2 * C * 16)
            stats(0, range(T, NT)).then_inc(s_tiles_stats, 1)
            ln_variance(0, 0)
            ln_rstd(0, 0)
            for q in range(Q):
                norm(0, 0, q)

            def add_out(g, r, q):
                dve.wait_ge(p_out, Q * g + q + 1)
                o = xin[r][:, 4 * q:4 * q + 4, :].rearrange("p t d -> p (t d)")
                V_.tensor_tensor(out=o, in0=bO[q % 2][:, :], in1=o, op=ALU.add).then_inc(v_out, 1)

            def group(i, k):
                g, s = R * i + k, k % 2
                more = not isinstance(g, int) or g < LAST
                if more:
                    nxt = (k + 1) % R
                    dve.wait_ge(s_x[nxt], 16 * filled(i, k + 1, R))
                    dve.wait_ge(s_ln, LN * (g + 1))
                    stats(nxt, range(T)).then_inc(s_tiles_stats, 1)
                    dve.wait_ge(s_src[1 - s], 2 * C * 16 * filled(i, k + 1, 2))
                    stats(nxt, range(T, NT)).then_inc(s_tiles_stats, 1)
                    wait(dve, s_ye, 2 * g)
                    wait(dve, s_y, Q * g)
                    ln_variance(g + 1, 1 - s)
                add_out(g, k % R, 0)
                dve.wait_ge(a_m, g + 1)
                wait(dve, v_run, g)
                dve.wait_ge(s_ea[s], 32 * filled(i, k, 2))
                last_col = CARRY_LAST if isinstance(g, int) and g == LAST else GE - 1
                V_.tensor_tensor_scan(run[s][:, :], mask[s][:, :], mT[:, :], run[1 - s][:, last_col:last_col + 1],
                                      ALU.mult, ALU.add).then_inc(v_run, 1)
                dve.wait_ge(p_pree, g + 1)
                dve.wait_ge(v_run, g + 1)
                wait(dve, a_ue, g)
                V_.tensor_tensor(out=preT[:, :].rearrange("d (c p) -> d c p", c=C),
                                 in0=bP[1][:, :].rearrange("d (c p) -> d c p", c=C),
                                 in1=run[s][:, :].rearrange("d (p c) -> d c p", c=C), op=ALU.add).then_inc(v_pree, 1)
                if more:
                    ln_rstd(g + 1, 1 - s)
                    wait(dve, p_hT, Q * g)
                    norm(g + 1, (k + 1) % R, 0)
                add_out(g, k % R, 1)
                if more:
                    for q in range(1, Q):
                        norm(g + 1, (k + 1) % R, q)
                add_out(g, k % R, 2)
                dve.wait_ge(p_oute, g + 1)
                o = xd[k % R][:, :, :]
                V_.tensor_tensor(out=o, in0=bE[:, :].rearrange("p (c d) -> p c d", c=C), in1=o, op=ALU.add).then_inc(v_oute, 1)
                add_out(g, k % R, 3)

            dve.wait_ge(v_init, 1)
            for k in range(R):
                group(0, k)
            with dve.Fori(1, LAST // R) as i:
                for k in range(R):
                    group(i, k)
            group(LAST // R, 0)

        @block.tensor
        def _(pe):
            mm = nc.tensor.matmul
            pe.wait_ge(s_ident, 3)
            pe.wait_ge(s_bad, 1)
            mm(bE[0:1, 0:1], bad_sum[:, 0:1], ones[0:G, 0:1], start=True, stop=True).then_inc(s_flag_ps, 1)
            pe.wait_ge(s_w, 160)
            nc.tensor.transpose(bM[:, 0:D], W2[:, :], ident[:, :]).then_inc(s_w2t_ps, 1)
            pe.wait_ge(s_w2t, 1)
            pe.wait_ge(s_flag, 1)
            mm(bE[:, 0:D], W2T[:, :], U1b[:, :], start=True, stop=True)
            mm(bE[:, D:D + 1], U1b[:, :], b2[:, 0:1], start=True, stop=True).then_inc(s_v_ps, 1)
            pe.wait_ge(s_idf, 3)
            for t, bank in ((sf, bT[0]), (df, bT[1]), (wf, bP[0])):
                for c in range(C):
                    last = nc.tensor.transpose(bank[:, c * G:(c + 1) * G],
                                               t[:, :].rearrange("g (p c) -> g c p", c=C)[:, c, :], ident[0:G, 0:G])
                last.then_inc(s_idx_ps, 1)
            pe.wait_ge(s_bad, 2)
            pe.wait_ge(s_v, 2)
            mm(bE[0:1, 256:257], bad_sum[:, 1:2], ones[0:G, 0:1], start=True, stop=True).then_inc(s_flag_ps, 1)

            def transposed(bank, tiles):
                for k, t in enumerate(tiles):
                    last = nc.tensor.transpose(bank[:, k * P:(k + 1) * P], t, ident[:, :])
                return last

            def quarter(s, q):
                return [y[s][:, k, :] for k in range(4 * q, 4 * q + 4)]

            def update(g, k, h):
                pe.wait_ge(a_hT, Q * g + k + 1)
                mm(bP[0][:, :], U1a[:, :], h[:, :], start=True, stop=True).then_inc(p_pre, 1)

            def bias(bank):
                mm(bank[:, :], ones3[:, :], c2_parts[:, :, :].rearrange("n a d -> n (a d)"), start=True, stop=False)

            def output(bank, u):
                for c in range(4):
                    last = mm(bank[:, c * D:(c + 1) * D], u[:, c, :], U2[:, :], start=False, stop=(c == 3))
                return last

            pe.wait_ge(s_c2, 8)
            pe.wait_ge(v_init, 2)
            pe.wait_ge(s_idx, 3)
            pe.wait_ge(s_y, 1)
            transposed(bT[0], quarter(0, 0)).then_inc(p_hT, 1)

            def group(i, k):
                g, s = R * i + k, k % 2
                more = not isinstance(g, int) or g < LAST
                pe.wait_ge(s_y, Q * g + 2)
                wait(pe, a_hT, Q * g)
                pe.wait_ge(s_ea[s], 32 * filled(i, k, 2))
                wait(pe, a_m, g)
                transposed(bT[1], quarter(s, 1)).then_inc(p_hT, 1)
                transposed(bM, [ea[s][:, c:c + 2, :].rearrange("p c d -> p (c d)") for c in range(0, C, 2)]).then_inc(p_ea, 1)
                pe.wait_ge(s_ye, 2 * g + 1)
                pe.wait_ge(a_hT, Q * g + 1)
                transposed(bT[0], [ys[s][:, c, :] for c in range(C)]).then_inc(p_hs, 1)
                wait(pe, a_u, Q * g)
                update(g, 0, hT[0])
                pe.wait_ge(s_y, Q * g + 3)
                pe.wait_ge(a_hT, Q * g + 2)
                transposed(bT[1], quarter(s, 2)).then_inc(p_hT, 1)
                wait(pe, v_pree, g)
                pe.wait_ge(a_hs, g + 1)
                mm(bP[1][:, :], W1a[:, :], hsT[:, :], start=True, stop=False)
                pe.wait_ge(a_ea, g + 1)
                mm(bP[1][:, :], W1b[:, :], eaT[:, :], start=False, stop=True).then_inc(p_z, 1)
                pe.wait_ge(a_u, Q * g + 1)
                update(g, 1, hT[1])
                wait(pe, v_out, Q * g)
                bias(bO[0])
                output(bO[0], uT[0]).then_inc(p_out, 1)
                pe.wait_ge(s_ye, 2 * g + 2)
                transposed(bT[0], [yd[s][:, c, :] for c in range(C)]).then_inc(p_hd, 1)
                pe.wait_ge(a_z, g + 1)
                mm(bM[:, :], V[:, :], zT[:, :], start=True, stop=True).then_inc(p_m, 1)
                pe.wait_ge(a_hd, g + 1)
                mm(bP[1][:, :], U1a[:, :], hdT[:, :], start=True, stop=True).then_inc(p_pree, 1)
                pe.wait_ge(s_y, Q * g + 4)
                pe.wait_ge(a_hT, Q * g + 3)
                transposed(bT[1], quarter(s, 3)).then_inc(p_hT, 1)
                pe.wait_ge(a_u, Q * g + 2)
                update(g, 2, hT[0])
                bias(bO[1])
                output(bO[1], uT[1]).then_inc(p_out, 1)
                pe.wait_ge(a_u, Q * g + 3)
                update(g, 3, hT[1])
                pe.wait_ge(v_out, Q * g + 1)
                bias(bO[0])
                output(bO[0], uT[2]).then_inc(p_out, 1)
                if more:
                    pe.wait_ge(s_y, Q * g + 5)
                    transposed(bT[0], quarter(1 - s, 0)).then_inc(p_hT, 1)
                wait(pe, v_oute, g)
                bias(bE)
                pe.wait_ge(a_ue, g + 1)
                output(bE, ueT).then_inc(p_oute, 1)
                pe.wait_ge(v_out, Q * g + 2)
                bias(bO[1])
                pe.wait_ge(a_u, Q * g + 4)
                output(bO[1], uT[3]).then_inc(p_out, 1)

            for k in range(R):
                group(0, k)
            with pe.Fori(1, LAST // R) as i:
                for k in range(R):
                    group(i, k)
            group(LAST // R, 0)


_INS = ['x', 'src', 'dst', 'edge_attr_64', 'L0_gnn_msg_w1', 'L0_gnn_msg_b1', 'L0_gnn_msg_w2', 'L0_gnn_msg_b2',
        'L0_gnn_upd_w1', 'L0_gnn_upd_b1', 'L0_gnn_upd_w2', 'L0_gnn_upd_b2']


def kernel(**inputs):
    import numpy as _np
    import concourse.bacc as _bacc
    from concourse import mybir as _mybir
    from concourse.bass_utils import run_bass_kernel_spmd as _run

    nc = _bacc.Bacc("TRN2", target_bir_lowering=False, num_devices=1)
    arrays, args = {}, []
    for name in _INS:
        a = _np.ascontiguousarray(inputs[name])
        arrays[f"in_{name}_dram"] = a
        args.append(nc.dram_tensor(f"in_{name}_dram", a.shape, _mybir.dt.from_np(a.dtype), kind="ExternalInput").ap())
    x = arrays["in_x_dram"]
    args.append(nc.dram_tensor("out_dram", x.shape, _mybir.dt.from_np(x.dtype), kind="ExternalOutput").ap())
    bass_preln_gnn(nc, *args)
    r = _run(nc, [arrays], core_ids=[0])
    return r.results[0]["out_dram"]
```

```python
import concourse.bass as bass
from concourse import mybir
from concourse.alu_op_type import AluOpType as ALU
from contextlib import ExitStack


def bass_preln_gnn(
    nc: bass.Bass,
    x: bass.AP,
    src: bass.AP,
    dst: bass.AP,
    edge_attr: bass.AP,
    msg_w1: bass.AP,
    msg_b1: bass.AP,
    msg_w2: bass.AP,
    msg_b2: bass.AP,
    upd_w1: bass.AP,
    upd_b1: bass.AP,
    upd_w2: bass.AP,
    upd_b2: bass.AP,
    out: bass.AP,
):
    f32 = mybir.dt.float32
    bf16 = mybir.dt.bfloat16
    i32 = mybir.dt.int32
    ACT = mybir.ActivationFunctionType
    AX = mybir.AxisListType

    NODES, D = x.shape
    EDGES, DE = edge_attr.shape
    EPS = 1e-5
    P = 128
    T = 16
    GN = P * T
    C = 4
    GE = P * C
    Q = T // 4
    G = -(-NODES // GN)
    LAST = G - 1
    R = 4
    QV = 2
    TV = 9
    assert 2 * DE == P and C == 4 and T == 16 and 8 < TV < 12
    assert G == -(-EDGES // GE) and LAST % R == 0
    NODE_LAST = NODES - GN
    EDGE_LAST = EDGES - GE
    CARRY_LAST = EDGE_LAST - 1 - (LAST - 1) * GE
    FAR = 1 << 20
    SQD = float(D) ** 0.5
    NT = T + 2 * C

    LN = 11
    NE = 6
    SB = 10
    SW = EDGES // SB
    FLAT = 4 * SW + (4 + SB) * GE + 2
    assert SW * SB == EDGES

    ctx = ExitStack()
    with ctx:
        def sb(name, shape, dt=f32):
            return ctx.enter_context(nc.sbuf_tensor(name, shape, dt))

        def ps(name):
            return ctx.enter_context(nc.psum_tensor(name, [P, 512], f32))

        def sem(name):
            return ctx.enter_context(nc.semaphore(name))

        mask_dram = nc.dram_tensor("mask_dram", [G, GE], bf16, kind="Internal").ap()
        src_sorted = nc.dram_tensor("src_sorted", [EDGES, 1], i32, kind="Internal").ap()
        dst_sorted = nc.dram_tensor("dst_sorted", [EDGES, 1], i32, kind="Internal").ap()
        erow_dram = nc.dram_tensor("erow_dram", [G * GE, D], f32, kind="Internal").ap()
        attr_sorted = nc.dram_tensor("attr_sorted", [EDGES, DE], f32, kind="Internal").ap()

        W1a, W1b = sb("W1a", [D, D]), sb("W1b", [DE, D])
        W2, W2T, U1b, V = sb("W2", [D, D]), sb("W2T", [D, D]), sb("U1b", [D, D]), sb("V", [D, D])
        U1a, U2 = sb("U1a", [D, D]), sb("U2", [D, D])
        b1, b2, c1, vb = sb("b1", [D, 1]), sb("b2", [D, 1]), sb("c1", [D, 1]), sb("vb", [D, 1])
        c2 = sb("c2", [3, D])
        c2_hi, c2_mid, c2_lo = (sb(n, [3, D], bf16) for n in ("c2_hi", "c2_mid", "c2_lo"))
        c2_rest, c2_rest2, c2_sum, c2_sum2 = (sb(n, [3, D]) for n in ("c2_rest", "c2_rest2", "c2_sum", "c2_sum2"))
        c2_parts = sb("c2_parts", [3, 4, D], bf16)
        ones3 = sb("ones3", [3, P], bf16)
        c2_rows = sb("c2_rows", [P, D])
        ident = sb("ident", [P, P])
        ones = sb("ones", [P, 1])
        pad = sb("pad", [1, 2])

        xin = [sb(f"xin{s}", [P, T, D]) for s in range(R)]
        y = [sb(f"y{s}", [P, T, D]) for s in range(2)]
        hT = [sb(f"hT{s}", [D, 512]) for s in range(2)]
        uT = [sb(f"uT{q}", [D, 4, P]) for q in range(Q)]

        xs = [sb(f"xs{s}", [P, C, D]) for s in range(2)]
        xd = [sb(f"xd{s}", [P, C, D]) for s in range(R)]
        ys = [sb(f"ys{s}", [P, C, D]) for s in range(2)]
        yd = [sb(f"yd{s}", [P, C, D]) for s in range(2)]
        ea = [sb(f"ea{s}", [P, C, DE]) for s in range(2)]
        mask = [sb(f"mask{s}", [P, GE], bf16) for s in range(2)]
        run = [sb(f"run{s}", [D, GE]) for s in range(2)]
        hsT, hdT, eaT = sb("hsT", [D, GE]), sb("hdT", [D, GE]), sb("eaT", [DE, GE])
        zT, mT, preT, ueT = sb("zT", [D, GE]), sb("mT", [D, GE]), sb("preT", [D, GE]), sb("ueT", [D, C, P])
        flat = sb("flat", [G, FLAT])

        st = sb("st", [P, NT, 6])
        st_sum, st_dif = sb("st_sum", [P, NT]), sb("st_dif", [P, NT])
        st_q, st_dd, st_v = sb("st_q", [P, NT]), sb("st_dd", [P, NT]), sb("st_v", [P, NT])
        st_root, st_r = sb("st_root", [P, NT]), sb("st_r", [P, NT])
        mean = [sb(f"mean{s}", [P, NT]) for s in range(2)]
        rstd = [sb(f"rstd{s}", [P, NT]) for s in range(2)]
        shift = [sb(f"shift{s}", [P, NT]) for s in range(2)]

        DEXT = FLAT - GE - 2
        dext = flat[0:G, DEXT:DEXT + GE + 2].bitcast(i32)
        d_prev, d_cur, d_next = dext[:, 0:GE], dext[:, 1:GE + 1], dext[:, 2:GE + 2]
        srow = ueT[0:G, :, :].rearrange("g c p -> g (c p)").bitcast(i32)
        gidx = sb("gidx", [G, 1], i32)
        bound = sb("bound", [G, 1])
        lastg = sb("lastg", [G, 1])
        far_flag = sb("far_flag", [G, 1])
        sf, df, wf = hsT[0:G, :], hdT[0:G, :], zT[0:G, :]
        same_next, bad = mT[0:G, :], preT[0:G, :]
        bad_sum = sb("bad_sum", [G, 2])
        mrow = sb("mrow", [G, GE], bf16)
        in_idx, out_idx = sb("in_idx", [P, G, 2, C], i32), sb("out_idx", [P, G, C], i32)
        g_idx = [sb(f"g_idx{s}", [P, 2, C], i32) for s in range(R)]
        o_idx = [sb(f"o_idx{s}", [P, C], i32) for s in range(R)]
        rank_col, src_col, dst_col = (o_idx[0][0:G, n:n + 1] for n in range(3))
        flags = sb("flags", [1, 2], i32)

        bT = [ps("bT0"), ps("bT1")]
        bP = [ps("bP0"), ps("bP1")]
        bO = [ps("bO0"), ps("bO1")]
        bM, bE = ps("bM"), ps("bE")

        s_x = [sem(f"s_x{s}") for s in range(R)]
        s_ea = [sem(f"s_ea{s}") for s in range(2)]
        s_src = [sem(f"s_src{s}") for s in range(2)]
        s_store = [sem(f"s_store{s}") for s in range(R)]
        s_erow = [sem(f"s_erow{s}") for s in range(R)]
        s_scat, s_back = sem("s_scat"), sem("s_back")
        s_w, s_dext, s_srow, s_mstore = sem("s_w"), sem("s_dext"), sem("s_srow"), sem("s_mstore")
        s_fill, s_ident, s_iota = sem("s_fill"), sem("s_ident"), sem("s_iota")
        s_idc, s_bad = sem("s_idc"), sem("s_bad")
        s_sorted_keys = sem("s_sorted_keys")
        s_flag_ps, s_flag = sem("s_flag_ps"), sem("s_flag")
        s_mrow, s_idf, s_idx_ps, s_idx = sem("s_mrow"), sem("s_idf"), sem("s_idx_ps"), sem("s_idx")
        s_w2t_ps, s_w2t, s_v_ps, s_v = sem("s_w2t_ps"), sem("s_w2t"), sem("s_v_ps"), sem("s_v")
        s_ln = sem("s_ln")
        s_root = sem("s_root")
        s_tiles_stats = sem("s_tiles_stats")
        s_y = sem("s_y")
        s_ye = sem("s_ye")
        s_y2, s_y3 = sem("s_y2"), sem("s_y3")
        s_rows = sem("s_rows")
        v_c2 = sem("v_c2")
        s_c2 = sem("s_c2")
        p_hT, p_ea, p_hs, p_hd = sem("p_hT"), sem("p_ea"), sem("p_hs"), sem("p_hd")
        p_pre, p_z, p_m, p_pree, p_out, p_oute = (sem(n) for n in ("p_pre", "p_z", "p_m", "p_pree", "p_out", "p_oute"))
        a_hT, a_ea, a_hs, a_hd, a_u, a_z, a_m, a_ue = (sem(n) for n in ("a_hT", "a_ea", "a_hs", "a_hd", "a_u", "a_z", "a_m", "a_ue"))
        v_run, v_pree, v_out, v_oute = sem("v_run"), sem("v_pree"), sem("v_out"), sem("v_oute")
        v_init = sem("v_init")
        r_blk, r_step, r_rank, r_row, r_scat, r_dma = (sem(n) for n in ("r_blk", "r_step", "r_rank", "r_row", "r_scat", "r_dma"))
        r_iota, r_col = sem("r_iota"), sem("r_col")
        s_gi, s_oi = sem("s_gi"), sem("s_oi")

        dst_blk = flat[0:G, 0:SW].bitcast(i32)
        pos_blk = flat[0:G, SW:2 * SW]
        cmp_a, cmp_b = flat[0:G, 2 * SW:3 * SW], flat[0:G, 3 * SW:4 * SW]
        base_f = 4 * SW
        own = flat[0:G, base_f:base_f + GE]
        own_b = flat[0:G, base_f + GE:base_f + 2 * GE]
        part = flat[0:G, base_f + 2 * GE:base_f + 2 * GE + SB * GE].rearrange("p (b c) -> p b c", b=SB)
        rank = flat[0:G, base_f + (2 + SB) * GE:base_f + (3 + SB) * GE].bitcast(i32)
        attr_row = cmp_a[:, 0:DE]

        def wait(eng, s, count):
            if not (isinstance(count, int) and count <= 0):
                eng.wait_ge(s, count)

        def filled(i, k, slots):
            return (R // slots) * i + k // slots + 1

        def node_rows(t, base):
            return t[bass.ds(base, GN), :].rearrange("(p t) d -> p t d", t=T)

        def attr_rows(t, base):
            return t[bass.ds(base, GE), :].rearrange("(p c) d -> p c d", c=C)

        def col(v):
            return v.rearrange("(n a) -> n a", a=1)

        W_LOADS = 11 * 16

        def plus_c2(eng, t):
            n = t.shape[1]
            return eng.tensor_tensor(out=t, in0=t, in1=c2_rows[:, :].rearrange("p (a d) -> p a d", a=1).to_broadcast([P, n, D]),
                                     op=ALU.add)

        block = ctx.enter_context(nc.Block())

        @block.sync
        def _(sp):
            def load_x(base, s):
                sp.dma_start(xin[s][:, :, :], node_rows(x, base)).then_inc(s_x[s], 16)

            def load_keys(d):
                mid = bass.AP(tensor=d.tensor, offset=d.offset + GE - 1, ap=[[GE, LAST - 1], [1, GE + 2]])
                sp.dma_start(dext[1:LAST, :], mid).then_inc(s_dext, 16)
                sp.dma_start(dext[0:1, 1:GE + 2], d[0:GE + 1].rearrange("(a n) -> a n", a=1)).then_inc(s_dext, 16)
                sp.dma_start(dext[LAST:G, 0:GE + 1], d[EDGE_LAST - 1:EDGES].rearrange("(a n) -> a n", a=1)).then_inc(s_dext, 16)

            def load_src(v):
                sp.dma_start(srow[0:LAST, :], v[0:LAST * GE].rearrange("(g n) -> g n", n=GE)).then_inc(s_srow, 16)
                sp.dma_start(srow[LAST:G, :], v[EDGE_LAST:EDGES].rearrange("(g n) -> g n", n=GE)).then_inc(s_srow, 16)

            sp.wait_ge(s_fill, 2)
            load_keys(dst)
            load_src(src)
            load_x(0, 0)

            sp.wait_ge(s_flag, 1)
            unsorted = sp.value_load(flags[0:1, 0:1])
            with sp.If(unsorted != 0):
                for b in range(SB):
                    if b:
                        sp.wait_ge(r_step, 4 * GE * b)
                    sp.dma_start(dst_blk, dst[b * SW:(b + 1) * SW].partition_broadcast(G)).then_inc(r_blk, 16)
                sp.wait_ge(r_rank, 1)

                def attr_column(c):
                    rest = edge_attr[0:LAST * GE, :].rearrange("(g n) d -> g n d", n=GE)[:, c, :]
                    sp.dma_start(attr_row[0:LAST, :], rest).then_inc(r_row, 16)
                    sp.dma_start(attr_row[LAST:G, :], edge_attr[bass.ds(c + EDGE_LAST, 1), :]).then_inc(r_row, 16)

                attr_column(0)
                with sp.Fori(1, GE) as c:
                    sp.wait_ge(r_scat, c * 48)
                    attr_column(c)
                sp.wait_ge(r_scat, GE * 48)
                load_keys(dst_sorted.rearrange("n a -> (n a)"))
                load_src(src_sorted.rearrange("n a -> (n a)"))
                sp.wait_ge(s_dext, 96)
                sp.wait_ge(s_srow, 64)
            sp.wait_ge(s_dext, 48)
            sp.wait_ge(s_srow, 32)
            sp.sem_inc(s_sorted_keys, 1)
            load_x(GN, 1)
            load_x(2 * GN, 2)

            sp.wait_ge(s_mrow, 1)
            sp.dma_start(mask_dram, mrow[:, :]).then_inc(s_mstore, 16)
            sp.wait_ge(s_mstore, 16)

            def load_edges(g, base, s):
                m = mask_dram[bass.ds(g, 1), :].rearrange("a n -> (a n)")
                sp.dma_start(mask[s][:, :], m.partition_broadcast(P)).then_inc(s_ea[s], 16)
                with sp.If(unsorted != 0):
                    sp.dma_start(ea[s][:, :, :], attr_rows(attr_sorted, base)).then_inc(s_ea[s], 16)
                with sp.If(unsorted == 0):
                    sp.dma_start(ea[s][:, :, :], attr_rows(edge_attr, base)).then_inc(s_ea[s], 16)

            load_edges(0, 0, 0)
            load_edges(1, GE, 1)

            def step(i, k):
                g = R * i + k
                static = isinstance(g, int)
                if not static or g + 3 <= LAST:
                    if not static or g > 0:
                        sp.wait_ge(s_store[(k - 1) % R], 16 * filled(i, k - 1, R))
                    load_x(NODE_LAST if static and g + 3 == LAST else (g + 3) * GN, (k + 3) % R)
                if not static or g + 2 <= LAST:
                    sp.wait_ge(p_ea, g + 1)
                    sp.wait_ge(v_run, g + 1)
                    load_edges(g + 2, EDGE_LAST if static and g + 2 == LAST else (g + 2) * GE, k % 2)
                sp.wait_ge(v_out, Q * (g + 1))
                sp.dma_start(node_rows(out, g * GN), xin[k % R][:, :, :]).then_inc(s_store[k % R], 16)

            def last_step():
                k = LAST % R
                last_before = (LAST - 1) % R
                sp.wait_ge(s_store[last_before], 16 * filled(0, LAST - 1, R))
                for q in range(Q):
                    sp.wait_ge(v_out, Q * LAST + q + 1)
                    sp.dma_start(node_rows(out, NODE_LAST)[:, 4 * q:4 * q + 4, :],
                                 xin[k][:, 4 * q:4 * q + 4, :]).then_inc(s_store[k], 16)

            for k in range(R):
                step(0, k)
            with sp.Fori(1, LAST // R - 1) as i:
                for k in range(R):
                    step(i, k)
            for k in range(R):
                step(LAST // R - 1, k)
            last_step()
            for k in range(R):
                sp.wait_ge(s_store[k], 16 * (LAST // R + Q * (k == 0)))

        @block.gpsimd
        def _(pool):
            def carry_wait(n=0):
                pool.tensor_tensor(out=pad[:, n:n + 1], in0=ident[0:1, 0:1], in1=ident[0:1, 0:1], op=ALU.add)

            pool.memset(dext[:, 0:1], -1).then_inc(s_fill, 1)
            pool.memset(dext[:, GE + 1:GE + 2], FAR).then_inc(s_fill, 1)
            pool.iota(gidx[:, :], pattern=[[0, 1]], base=0, channel_multiplier=1).then_inc(s_iota, 1)
            pool.memset(ident[:, :], 0.0).then_inc(s_ident, 1)
            pool.memset(ones[:, :], 1.0).then_inc(s_ident, 1)
            pool.wait_ge(s_ident, 2)
            pool.affine_select(out=ident[:, :], in_=ident[:, :], compare_op=ALU.not_equal, fill=1.0,
                               base=0, pattern=[[-1, P]], channel_multiplier=1).then_inc(s_ident, 1)
            pool.wait_ge(s_ident, 3)

            pool.wait_ge(s_flag, 1)
            unsorted = pool.value_load(flags[0:1, 0:1])
            with pool.If(unsorted != 0):
                pool.iota(pos_blk, pattern=[[1, SW]], base=0, channel_multiplier=0,
                          allow_small_or_imprecise_dtypes=True).then_inc(r_iota, 1)
                pool.iota(own, pattern=[[1, GE]], base=0, channel_multiplier=0,
                          allow_small_or_imprecise_dtypes=True).then_inc(r_iota, 1)
                pool.wait_ge(r_rank, 1)
                pool.wait_ge(s_srow, 32)
                with pool.Fori(0, GE) as c:
                    pool.wait_ge(r_row, (c + 1) * 32)
                    pool.tensor_copy(rank_col, rank[:, bass.ds(c, 1)]).then_inc(r_col, 1)
                    pool.tensor_copy(src_col, srow[:, bass.ds(c, 1)]).then_inc(r_col, 1)
                    pool.tensor_copy(dst_col, dext[:, bass.ds(c + 1, 1)]).then_inc(r_col, 1)
                    pool.wait_ge(r_col, 3 * (c + 1))
                    carry_wait()
                    off = bass.IndirectOffsetOnAxis(rank_col, 0)
                    pool.indirect_dma_start(attr_sorted, off, attr_row, None).then_inc(r_scat, 16)
                    pool.indirect_dma_start(src_sorted, off, src_col, None).then_inc(r_scat, 16)
                    pool.indirect_dma_start(dst_sorted, off, dst_col, None).then_inc(r_scat, 16)
                    pool.wait_ge(r_scat, (c + 1) * 48)
                    carry_wait(1)

            def indices(g, r):
                pool.tensor_copy(g_idx[r][:, :, :], in_idx[:, bass.ds(g, 1), :, :].rearrange("p a n c -> p (a n) c")).then_inc(s_gi, 1)

            def gather(n, t, s, r):
                for c in range(C):
                    pool.indirect_dma_start(t[:, c, :], None, x,
                                            bass.IndirectOffsetOnAxis(g_idx[r][:, n, c:c + 1], 0)).then_inc(s_src[s], 16)

            def row_indices(g, s):
                pool.tensor_copy(o_idx[s][:, :], out_idx[:, g, :]).then_inc(s_oi, 1)
                pool.wait_ge(s_oi, g + 1)
                carry_wait()

            def scatter(s, done):
                for c in range(C):
                    pool.indirect_dma_start(out, bass.IndirectOffsetOnAxis(o_idx[s][:, c:c + 1], 0),
                                            xd[s][:, c, :], None,
                                            bounds_check=NODES - 1, oob_is_err=False).then_inc(done, 16)

            pool.wait_ge(s_idx, 2)
            indices(0, 0)
            indices(1, 1)
            pool.wait_ge(s_gi, 2)
            for k in range(2):
                gather(0, xs[k], k, k)
                gather(1, xd[k], k, k)
            pool.wait_ge(s_idx, 3)
            pool.wait_ge(s_w, W_LOADS)
            pool.wait_ge(s_flag, 2)
            late = pool.value_load(flags[0:1, 1:2])

            def step(i, k):
                g = R * i + k
                static = isinstance(g, int)
                if not static or g + 2 <= LAST:
                    indices(g + 2, (k + 2) % R)
                    pool.wait_ge(s_ye, 2 * g + 1)
                    pool.wait_ge(s_gi, g + 3)
                    carry_wait()
                    gather(0, xs[k % 2], k % 2, (k + 2) % R)
                    if not static or g >= 2:
                        pool.wait_ge(s_erow[(k - 2) % R], C * 16 * filled(i, k - 2, R))
                pool.wait_ge(s_ye, 2 * (g + 1))
                plus_c2(pool, xd[k % R][:, :, :]).then_inc(s_rows, 1)
                if not static or g + 2 <= LAST:
                    gather(1, xd[(k + 2) % R], k % 2, (k + 2) % R)
                if not static or g > 0:
                    p = (k - 1) % R
                    pool.wait_ge(v_oute, g)
                    pool.wait_ge(s_store[p], 16 * filled(i, k - 1, R))
                    row_indices(g - 1, p)
                    with pool.If(late == 0):
                        scatter(p, s_erow[p])
                    with pool.If(late != 0):
                        for c in range(C):
                            pool.dma_start(erow_dram[bass.ds((g - 1) * GE + c * P, P), :],
                                           xd[p][:, c, :]).then_inc(s_erow[p], 16)

            for k in range(R):
                step(0, k)
            with pool.Fori(1, LAST // R - 1) as i:
                for k in range(R):
                    step(i, k)
            for k in range(R):
                step(LAST // R - 1, k)
            step(LAST // R, 0)
            pool.wait_ge(v_oute, G)
            row_indices(LAST, 0)
            pool.wait_ge(s_store[0], 16 * (LAST // R + Q))
            for k in range(R):
                pool.wait_ge(s_erow[k], C * 16 * (LAST // R))
            scatter(0, s_scat)
            pool.wait_ge(s_scat, 16 * C)
            with pool.If(late != 0):
                with pool.Fori(0, LAST) as g:
                    pool.tensor_copy(o_idx[0][:, :], out_idx[:, g, :]).then_inc(s_oi, 1)
                    for c in range(C):
                        pool.dma_start(xd[0][:, c, :], erow_dram[bass.ds(g * GE + c * P, P), :]).then_inc(s_back, 16)
                    pool.wait_ge(s_back, 16 * C * (g + 1))
                    pool.wait_ge(s_oi, G + g + 1)
                    carry_wait()
                    scatter(0, s_scat)
                    pool.wait_ge(s_scat, 16 * C * (g + 2))
                    carry_wait(1)

        @block.scalar
        def _(act):
            def relu_scaled(o, i):
                return nc.scalar.activation(o, i, ACT.Relu, scale=SQD)

            def norm_tiles(s, r, js):
                for j in js:
                    last = nc.scalar.activation(y[s][:, j, :], xin[r][:, j, :], ACT.Identity,
                                                scale=rstd[s][:, j:j + 1], bias=shift[s][:, j:j + 1])
                    if j == 3 * T // 4 - 1:
                        last.then_inc(s_y2, 1)
                    if j == T - 1:
                        last.then_inc(s_y3, 1)

            def norm_edges(s, r, js):
                for j in js:
                    t, tile, k = (xs[s], ys, j) if j < C else (xd[r], yd, j - C)
                    last = nc.scalar.activation(tile[s][:, k, :], t[:, k, :], ACT.Identity,
                                                scale=rstd[s][:, T + j:T + j + 1], bias=shift[s][:, T + j:T + j + 1])
                    if k == C - 1:
                        last.then_inc(s_ye, 1)

            act.wait_ge(s_dext, 48)
            for t, v in ((W2, msg_w2), (U1b, upd_w1[D:2 * D, :]), (b2, col(msg_b2)), (b1, col(msg_b1)), (c1, col(upd_b1)),
                         (W1a, msg_w1[0:D, :]), (W1b, msg_w1[D:D + DE, :]), (U1a, upd_w1[0:D, :]), (U2, upd_w2),
                         (c2, upd_b2.partition_broadcast(3)), (c2_rows, upd_b2.partition_broadcast(P))):
                act.dma_start(t[:, :], v).then_inc(s_w, 16)

            def root(chain, j=slice(0, NT)):
                act.wait_ge(s_ln, LN * chain + 6)
                nc.scalar.activation(st_root[:, j], st_v[:, j], ACT.Sqrt).then_inc(s_root, 1)

            root(0, slice(0, T))
            act.wait_ge(s_w2t_ps, 1)
            nc.scalar.activation(W2T[:, :], bM[:, 0:D], ACT.Copy).then_inc(s_w2t, 1)
            act.wait_ge(s_v_ps, 1)
            nc.scalar.activation(V[:, :], bE[:, 0:D], ACT.Copy).then_inc(s_v, 1)
            nc.scalar.activation(vb[:, :], bE[:, D:D + 1], ACT.Copy).then_inc(s_v, 1)
            act.wait_ge(s_v, 2)
            act.wait_ge(s_w, W_LOADS)

            act.wait_ge(p_hT, 1)
            relu_scaled(hT[0][:, :], bT[0][:, :]).then_inc(a_hT, 1)
            act.wait_ge(s_ln, LN)
            norm_tiles(0, 0, range(TV, T - 4))
            root(1, slice(T, NT))
            act.wait_ge(s_ln, 2 * LN)
            norm_edges(0, 0, range(NE))

            def evac_u(g, k):
                act.wait_ge(p_pre, Q * g + k + 1)
                nc.scalar.activation(uT[k][:, :, :].rearrange("d c p -> d (c p)"), bP[0][:, :], ACT.Relu,
                                     bias=c1[:, 0:1]).then_inc(a_u, 1)

            def group(i, k):
                g, s = R * i + k, k % 2
                more = not isinstance(g, int) or g < LAST
                act.wait_ge(p_hT, Q * g + 2)
                relu_scaled(hT[1][:, :], bT[1][:, :]).then_inc(a_hT, 1)
                act.wait_ge(p_ea, g + 1)
                for h in range(2):
                    last = nc.scalar.activation(eaT[:, :].rearrange("d (j h p) -> d h j p", j=2, h=2)[:, h, :, :],
                                                bM[h * DE:(h + 1) * DE, 0:2 * P].rearrange("d (j p) -> d j p", j=2), ACT.Copy)
                last.then_inc(a_ea, 1)
                act.wait_ge(p_hs, g + 1)
                relu_scaled(hsT[:, :], bT[0][:, :]).then_inc(a_hs, 1)
                evac_u(g, 0)
                act.wait_ge(p_hT, Q * g + 3)
                relu_scaled(hT[0][:, :], bT[1][:, :]).then_inc(a_hT, 1)
                norm_edges(s, k % R, range(NE, 2 * C))
                norm_tiles(s, k % R, range(T - 4, T - 3))
                act.wait_ge(p_z, g + 1)
                nc.scalar.activation(zT[:, :], bP[1][:, :], ACT.Relu, bias=b1[:, 0:1]).then_inc(a_z, 1)
                evac_u(g, 1)
                norm_tiles(s, k % R, range(T - 3, T - 2))
                act.wait_ge(p_hd, g + 1)
                relu_scaled(hdT[:, :], bT[0][:, :]).then_inc(a_hd, 1)
                norm_tiles(s, k % R, range(T - 2, T - 1))
                act.wait_ge(p_m, g + 1)
                wait(act, v_run, g)
                nc.scalar.activation(mT[:, :].rearrange("d (p c) -> d c p", c=C),
                                     bM[:, :].rearrange("d (c p) -> d c p", c=C), ACT.Identity,
                                     bias=vb[:, 0:1]).then_inc(a_m, 1)
                if more:
                    root(g + 2)
                norm_tiles(s, k % R, range(T - 1, T))
                evac_u(g, 2)
                act.wait_ge(p_hT, Q * g + 4)
                relu_scaled(hT[1][:, :], bT[1][:, :]).then_inc(a_hT, 1)
                act.wait_ge(v_pree, g + 1)
                nc.scalar.activation(ueT[:, :, :].rearrange("d c p -> d (c p)"), preT[:, :], ACT.Relu,
                                     bias=c1[:, 0:1]).then_inc(a_ue, 1)
                if more:
                    act.wait_ge(s_ln, LN * (g + 3))
                    norm_edges(1 - s, (k + 1) % R, range(0, C))
                evac_u(g, 3)
                if more:
                    norm_edges(1 - s, (k + 1) % R, range(C, NE))
                    act.wait_ge(p_hT, Q * g + 5)
                    relu_scaled(hT[0][:, :], bT[0][:, :]).then_inc(a_hT, 1)
                    norm_tiles(1 - s, (k + 1) % R, range(TV, T - 4))

            for k in range(R):
                group(0, k)
            with act.Fori(1, LAST // R) as i:
                for k in range(R):
                    group(i, k)
            group(LAST // R, 0)

        @block.vector
        def _(dve):
            nc.vector.memset(run[1][:, :], 0.0).then_inc(v_init, 1)
            nc.vector.memset(ones3[:, :], 1.0).then_inc(v_init, 1)

            def stats(r, js):
                for j in js:
                    t, k = (xin[r], j) if j < T else (xs[r % 2], j - T) if j < T + C else (xd[r], j - T - C)
                    last = nc.vector.bn_stats(st[:, j, :], t[:, k, :])
                return last

            dve.wait_ge(s_dext, 48)
            dve.wait_ge(s_fill, 2)
            nc.vector.tensor_tensor(out=bad[:, :], in0=d_cur, in1=d_next, op=ALU.is_gt).then_inc(s_idc, 1)
            dve.wait_ge(s_idc, 1)
            nc.vector.reduce_sum(bad_sum[:, 0:1], bad[:, :], axis=AX.X).then_inc(s_bad, 1)
            dve.wait_ge(s_flag_ps, 1)
            nc.vector.tensor_copy(flags[0:1, 0:1], bE[0:1, 0:1]).then_inc(s_flag, 1)

            dve.wait_ge(s_flag, 1)
            unsorted = dve.value_load(flags[0:1, 0:1])
            with dve.If(unsorted != 0):
                dve.wait_ge(r_iota, 2)
                dve.wait_ge(s_iota, 1)
                nc.vector.tensor_copy(df[:, :], d_cur).then_inc(r_dma, 1)
                nc.vector.tensor_scalar(bound[:, :], gidx[:, :], float(GE), float(EDGE_LAST), ALU.mult, ALU.min).then_inc(r_dma, 1)
                dve.wait_ge(r_dma, 2)
                nc.vector.tensor_scalar(own, own, bound[:, 0:1], None, ALU.add).then_inc(r_dma, 1)
                dve.wait_ge(r_dma, 3)
                for b in range(SB):
                    dve.wait_ge(r_blk, 16 * (b + 1))
                    nc.vector.tensor_scalar(own_b, own, float(b * SW), None, ALU.subtract).then_inc(r_dma, 1)
                    dve.wait_ge(r_dma, b + 4)
                    def count_column(c):
                        n = c * 4 + b * 4 * GE
                        wait(dve, r_step, n)
                        nc.vector.tensor_scalar(cmp_a, dst_blk, df[:, bass.ds(c, 1)], 32768.0, ALU.subtract, ALU.mult).then_inc(r_step, 1)
                        dve.wait_ge(r_step, n + 1)
                        nc.vector.scalar_tensor_tensor(out=cmp_b, in0=cmp_a, scalar=own_b[:, bass.ds(c, 1)], in1=pos_blk,
                                                       op0=ALU.subtract, op1=ALU.add).then_inc(r_step, 1)
                        dve.wait_ge(r_step, n + 2)
                        nc.vector.tensor_scalar(cmp_a, cmp_b, 0.0, None, ALU.is_lt).then_inc(r_step, 1)
                        dve.wait_ge(r_step, n + 3)
                        nc.vector.reduce_sum(part[:, b, bass.ds(c, 1)], cmp_a, axis=AX.X).then_inc(r_step, 1)

                    count_column(0)
                    with dve.Fori(1, GE) as c:
                        count_column(c)
                    dve.wait_ge(r_step, (b + 1) * 4 * GE)
                nc.vector.reduce_sum(own_b, part.rearrange("p b c -> p c b"), axis=AX.X).then_inc(r_dma, 1)
                dve.wait_ge(r_dma, SB + 4)
                nc.vector.tensor_copy(rank, own_b).then_inc(r_rank, 1)

            dve.wait_ge(s_sorted_keys, 1)
            dve.wait_ge(s_iota, 1)
            V_ = nc.vector
            V_.tensor_copy(sf[:, :], srow[:, :]).then_inc(s_idf, 1)
            V_.tensor_copy(df[:, :], d_cur).then_inc(s_idf, 1)
            V_.tensor_tensor(out=same_next[:, :], in0=d_cur, in1=d_next, op=ALU.is_equal).then_inc(s_idc, 1)
            V_.tensor_tensor(out=mrow[:, :], in0=d_cur, in1=d_prev, op=ALU.is_equal).then_inc(s_mrow, 1)
            def index_table(n, t, bank):
                dve.wait_ge(s_idx_ps, n + 1)
                V_.tensor_copy(t.rearrange("p g c -> p c g"),
                               bank[:, 0:C * G].rearrange("p (c g) -> p c g", c=C)).then_inc(s_idx, 1)

            index_table(0, in_idx[:, :, 0, :], bT[0])
            index_table(1, in_idx[:, :, 1, :], bT[1])
            V_.tensor_scalar(bound[:, :], gidx[:, :], float(GN), float(GN), ALU.mult, ALU.add).then_inc(s_idc, 1)
            V_.tensor_scalar(lastg[:, :], gidx[:, :], float(LAST), float(FAR), ALU.is_equal, ALU.mult).then_inc(s_idc, 1)
            dve.wait_ge(s_idc, 4)
            V_.tensor_scalar(bound[:, :], bound[:, :], float(NODE_LAST), lastg[:, 0:1], ALU.min, ALU.add).then_inc(s_idc, 1)
            dve.wait_ge(s_idf, 2)
            V_.scalar_tensor_tensor(out=wf[:, :], in0=same_next[:, :], scalar=float(FAR), in1=df[:, :],
                                    op0=ALU.mult, op1=ALU.add).then_inc(s_idf, 1)
            dve.wait_ge(s_idc, 5)
            V_.tensor_scalar(bad[:, :], df[:, :], bound[:, 0:1], None, ALU.is_ge).then_inc(s_idc, 1)
            dve.wait_ge(s_idc, 6)
            V_.reduce_sum(bad_sum[:, 1:2], bad[:, :], axis=AX.X).then_inc(s_bad, 1)
            index_table(2, out_idx[:, :, :], bP[0])
            dve.wait_ge(s_flag_ps, 2)
            V_.tensor_copy(flags[0:1, 1:2], bO[1][0:1, 0:1]).then_inc(s_flag, 1)

            def ln_variance(chain, s, j=slice(0, NT)):
                n = LN * chain
                dve.wait_ge(s_tiles_stats, 1 if j.stop == T else 2 * chain)
                V_.tensor_tensor(out=st_dif[:, j], in0=st[:, j, 1], in1=st[:, j, 4], op=ALU.subtract).then_inc(s_ln, 1)
                V_.scalar_tensor_tensor(out=st_q[:, j], in0=st[:, j, 2], scalar=float(D) * EPS, in1=st[:, j, 5],
                                        op0=ALU.add, op1=ALU.add).then_inc(s_ln, 1)
                V_.tensor_tensor(out=st_sum[:, j], in0=st[:, j, 1], in1=st[:, j, 4], op=ALU.add).then_inc(s_ln, 1)
                dve.wait_ge(s_ln, n + 1)
                V_.tensor_tensor(out=st_dd[:, j], in0=st_dif[:, j], in1=st_dif[:, j], op=ALU.mult).then_inc(s_ln, 1)
                dve.wait_ge(s_ln, n + 3)
                V_.tensor_scalar(mean[s][:, j], st_sum[:, j], 0.5, None, ALU.mult).then_inc(s_ln, 1)
                dve.wait_ge(s_ln, n + 4)
                V_.scalar_tensor_tensor(out=st_v[:, j], in0=st_dd[:, j], scalar=float(D) / 4, in1=st_q[:, j],
                                        op0=ALU.mult, op1=ALU.add).then_inc(s_ln, 1)

            def ln_inverse(chain, j=slice(0, NT)):
                dve.wait_ge(s_root, chain + 1)
                V_.reciprocal(st_r[:, j], st_root[:, j]).then_inc(s_ln, 1)

            def ln_newton1(chain, j=slice(0, NT)):
                dve.wait_ge(s_ln, LN * chain + 7)
                V_.scalar_tensor_tensor(out=st_dd[:, j], in0=st_r[:, j], scalar=-0.5, in1=st_r[:, j],
                                        op0=ALU.mult, op1=ALU.mult).then_inc(s_ln, 1)

            def ln_newton2(chain, j=slice(0, NT)):
                dve.wait_ge(s_ln, LN * chain + 8)
                V_.tensor_tensor(out=st_q[:, j], in0=st_dd[:, j], in1=st_v[:, j], op=ALU.mult).then_inc(s_ln, 1)

            def ln_rstd(chain, s, j=slice(0, NT)):
                dve.wait_ge(s_ln, LN * chain + 9)
                V_.scalar_tensor_tensor(out=rstd[s][:, j], in0=st_q[:, j], scalar=1.5, in1=st_r[:, j],
                                        op0=ALU.add, op1=ALU.mult).then_inc(s_ln, 1)

            def ln_shift(chain, s, j=slice(0, NT)):
                dve.wait_ge(s_ln, LN * chain + 10)
                V_.scalar_tensor_tensor(out=shift[s][:, j], in0=mean[s][:, j], scalar=-1.0, in1=rstd[s][:, j],
                                        op0=ALU.mult, op1=ALU.mult).then_inc(s_ln, 1)

            def with_c2(g, r):
                dve.wait_ge(s_y, (Q - 1) * g + QV)
                dve.wait_ge(s_w, W_LOADS)
                plus_c2(nc.vector, xin[r][:, 0:4 * QV, :]).then_inc(v_c2, 1)

            def norm_tile(s, r, k):
                return V_.tensor_scalar(y[s][:, k, :], xin[r][:, k, :], mean[s][:, k:k + 1], rstd[s][:, k:k + 1],
                                        ALU.subtract, ALU.mult)

            def norm(g, r, q, start=None):
                s = r % 2
                start = 4 * q if start is None else start
                for k in range(start, min(4 * q + 4, TV)):
                    last = norm_tile(s, r, k)
                last.then_inc(s_y, 1)

            dense_tiles = slice(0, T)
            dve.wait_ge(s_x[0], 16)
            stats(0, range(T)).then_inc(s_tiles_stats, 1)
            ln_variance(0, 0, dense_tiles)
            ln_inverse(0, dense_tiles)
            ln_newton1(0, dense_tiles)
            ln_newton2(0, dense_tiles)
            ln_rstd(0, 0, dense_tiles)
            ln_shift(0, 0, dense_tiles)
            dve.wait_ge(s_ln, LN - 1)
            for q in range(Q - 1):
                norm(0, 0, q)

            dve.wait_ge(s_src[0], 2 * C * 16)
            edge_tiles = slice(T, NT)
            stats(0, range(T, NT)).then_inc(s_tiles_stats, 1)
            ln_variance(1, 0, edge_tiles)
            ln_inverse(1, edge_tiles)
            ln_newton1(1, edge_tiles)
            ln_newton2(1, edge_tiles)
            ln_rstd(1, 0, edge_tiles)
            ln_shift(1, 0, edge_tiles)

            dve.wait_ge(s_w, W_LOADS)
            dve.wait_ge(s_ident, 2)
            V_.tensor_copy(c2_hi[:, :], c2[:, :]).then_inc(s_c2, 1)
            dve.wait_ge(s_c2, 1)
            V_.tensor_tensor(out=c2_rest[:, :], in0=c2[:, :], in1=c2_hi[:, :], op=ALU.subtract).then_inc(s_c2, 1)
            dve.wait_ge(s_c2, 2)
            V_.tensor_copy(c2_mid[:, :], c2_rest[:, :]).then_inc(s_c2, 1)
            dve.wait_ge(s_c2, 3)
            V_.tensor_tensor(out=c2_rest2[:, :], in0=c2_rest[:, :], in1=c2_mid[:, :], op=ALU.subtract).then_inc(s_c2, 1)
            dve.wait_ge(s_c2, 4)
            V_.tensor_copy(c2_lo[:, :], c2_rest2[:, :]).then_inc(s_c2, 1)
            dve.wait_ge(s_ident, 3)
            V_.tensor_scalar(c2_sum[:, :], c2_hi[:, :], ident[0:3, 0:1], None, ALU.mult).then_inc(s_c2, 1)
            dve.wait_ge(s_c2, 6)
            V_.scalar_tensor_tensor(out=c2_sum2[:, :], in0=c2_mid[:, :], scalar=ident[0:3, 1:2], in1=c2_sum[:, :],
                                    op0=ALU.mult, op1=ALU.add).then_inc(s_c2, 1)
            dve.wait_ge(s_c2, 7)
            for n in range(4):
                last = V_.scalar_tensor_tensor(out=c2_parts[:, n, :], in0=c2_lo[:, :], scalar=ident[0:3, 2:3],
                                               in1=c2_sum2[:, :], op0=ALU.mult, op1=ALU.add)
            last.then_inc(s_c2, 1)
            with_c2(0, 0)

            def add_out(g, r, q):
                dve.wait_ge(p_out, Q * g + q + 1)
                if q == 0:
                    dve.wait_ge(v_c2, g + 1)
                if q >= 2:
                    dve.wait_ge((s_y2, s_y3)[q - 2], g + 1)
                o = xin[r][:, 4 * q:4 * q + 4, :].rearrange("p t d -> p (t d)")
                V_.tensor_tensor(out=o, in0=bO[q % 2][:, :], in1=o, op=ALU.add).then_inc(v_out, 1)

            def group(i, k):
                g, s = R * i + k, k % 2
                more = not isinstance(g, int) or g < LAST
                if more:
                    nxt = (k + 1) % R
                    dve.wait_ge(s_x[nxt], 16 * filled(i, k + 1, R))
                    dve.wait_ge(s_ln, LN * (g + 2))
                    stats(nxt, range(T)).then_inc(s_tiles_stats, 1)
                    dve.wait_ge(s_src[1 - s], 2 * C * 16 * filled(i, k + 1, 2))
                    stats(nxt, range(T, NT)).then_inc(s_tiles_stats, 1)
                    wait(dve, s_ye, 2 * g)
                    wait(dve, s_y, (Q - 1) * g)
                    wait(dve, s_y3, g)
                add_out(g, k % R, 0)
                if more:
                    ln_variance(g + 2, 1 - s)
                dve.wait_ge(a_m, g + 1)
                wait(dve, v_run, g)
                dve.wait_ge(s_ea[s], 32 * filled(i, k, 2))
                last_col = CARRY_LAST if isinstance(g, int) and g == LAST else GE - 1
                V_.tensor_tensor_scan(run[s][:, :], mask[s][:, :], mT[:, :], run[1 - s][:, last_col:last_col + 1],
                                      ALU.mult, ALU.add).then_inc(v_run, 1)
                if more:
                    ln_inverse(g + 2)
                dve.wait_ge(p_pree, g + 1)
                dve.wait_ge(v_run, g + 1)
                wait(dve, a_ue, g)
                V_.tensor_tensor(out=preT[:, :].rearrange("d (c p) -> d c p", c=C),
                                 in0=bP[1][:, :].rearrange("d (c p) -> d c p", c=C),
                                 in1=run[s][:, :].rearrange("d (p c) -> d c p", c=C), op=ALU.add).then_inc(v_pree, 1)
                if more:
                    ln_newton1(g + 2)
                    ln_newton2(g + 2)
                if more:
                    ln_rstd(g + 2, 1 - s)
                    wait(dve, p_hT, Q * g)
                    dve.wait_ge(s_ln, LN * (g + 3) - 1)
                    norm_tile(1 - s, (k + 1) % R, 0)
                    ln_shift(g + 2, 1 - s)
                    norm(g + 1, (k + 1) % R, 0, 1)
                add_out(g, k % R, 1)
                if more:
                    norm(g + 1, (k + 1) % R, 1)
                    norm(g + 1, (k + 1) % R, 2)
                    with_c2(g + 1, (k + 1) % R)
                add_out(g, k % R, 2)
                if not more:
                    add_out(g, k % R, 3)
                dve.wait_ge(p_oute, g + 1)
                dve.wait_ge(s_rows, g + 1)
                o = xd[k % R][:, :, :]
                V_.tensor_tensor(out=o, in0=bE[:, :].rearrange("p (c d) -> p c d", c=C), in1=o, op=ALU.add).then_inc(v_oute, 1)
                if more:
                    add_out(g, k % R, 3)

            dve.wait_ge(v_init, 1)
            for k in range(R):
                group(0, k)
            with dve.Fori(1, LAST // R) as i:
                for k in range(R):
                    group(i, k)
            group(LAST // R, 0)

        @block.tensor
        def _(pe):
            mm = nc.tensor.matmul
            pe.wait_ge(s_ident, 3)
            pe.wait_ge(s_bad, 1)
            mm(bE[0:1, 0:1], bad_sum[:, 0:1], ones[0:G, 0:1], start=True, stop=True).then_inc(s_flag_ps, 1)
            for n, (t, bank) in enumerate(((sf, bT[0]), (df, bT[1]), (wf, bP[0]))):
                pe.wait_ge(s_idf, n + 1)
                for c in range(C):
                    last = nc.tensor.transpose(bank[:, c * G:(c + 1) * G],
                                               t[:, :].rearrange("g (p c) -> g c p", c=C)[:, c, :], ident[0:G, 0:G])
                last.then_inc(s_idx_ps, 1)
            pe.wait_ge(s_bad, 2)
            mm(bO[1][0:1, 0:1], bad_sum[:, 1:2], ones[0:G, 0:1], start=True, stop=True).then_inc(s_flag_ps, 1)
            pe.wait_ge(s_w, W_LOADS)
            nc.tensor.transpose(bM[:, 0:D], W2[:, :], ident[:, :]).then_inc(s_w2t_ps, 1)
            pe.wait_ge(s_w2t, 1)
            pe.wait_ge(s_flag, 1)
            mm(bE[:, 0:D], W2T[:, :], U1b[:, :], start=True, stop=True)
            mm(bE[:, D:D + 1], U1b[:, :], b2[:, 0:1], start=True, stop=True).then_inc(s_v_ps, 1)

            def transposed(bank, tiles):
                for k, t in enumerate(tiles):
                    last = nc.tensor.transpose(bank[:, k * P:(k + 1) * P], t, ident[:, :])
                return last

            def quarter(s, q):
                return [y[s][:, k, :] for k in range(4 * q, 4 * q + 4)]

            def update(g, k, h):
                pe.wait_ge(a_hT, Q * g + k + 1)
                mm(bP[0][:, :], U1a[:, :], h[:, :], start=True, stop=True).then_inc(p_pre, 1)

            def bias(bank, g):
                if isinstance(g, int) and g == 0:
                    pe.wait_ge(s_c2, 8)
                    pe.wait_ge(v_init, 2)
                mm(bank[:, :], ones3[:, :], c2_parts[:, :, :].rearrange("n a d -> n (a d)"), start=True, stop=False)

            def output(bank, u, biased):
                for c in range(4):
                    last = mm(bank[:, c * D:(c + 1) * D], u[:, c, :], U2[:, :], start=not biased, stop=not biased or c == 3)
                return last

            pe.wait_ge(s_idx, 3)
            pe.wait_ge(s_y, 1)
            transposed(bT[0], quarter(0, 0)).then_inc(p_hT, 1)
            pe.wait_ge(s_v, 2)
            pe.wait_ge(s_flag, 2)

            def group(i, k):
                g, s = R * i + k, k % 2
                more = not isinstance(g, int) or g < LAST
                pe.wait_ge(s_y, (Q - 1) * g + 2)
                wait(pe, a_hT, Q * g)
                pe.wait_ge(s_ea[s], 32 * filled(i, k, 2))
                wait(pe, a_m, g)
                transposed(bT[1], quarter(s, 1)).then_inc(p_hT, 1)
                transposed(bM, [ea[s][:, c:c + 2, :].rearrange("p c d -> p (c d)") for c in range(0, C, 2)]).then_inc(p_ea, 1)
                wait(pe, a_u, Q * g)
                update(g, 0, hT[0])
                pe.wait_ge(s_ye, 2 * g + 1)
                pe.wait_ge(a_hT, Q * g + 1)
                transposed(bT[0], [ys[s][:, c, :] for c in range(C)]).then_inc(p_hs, 1)
                pe.wait_ge(s_y, (Q - 1) * g + 3)
                pe.wait_ge(s_y2, g + 1)
                pe.wait_ge(a_hT, Q * g + 2)
                transposed(bT[1], quarter(s, 2)).then_inc(p_hT, 1)
                wait(pe, v_pree, g)
                pe.wait_ge(a_ea, g + 1)
                mm(bP[1][:, :], W1b[:, :], eaT[:, :], start=True, stop=False)
                pe.wait_ge(a_hs, g + 1)
                mm(bP[1][:, :], W1a[:, :], hsT[:, :], start=False, stop=True).then_inc(p_z, 1)
                pe.wait_ge(a_u, Q * g + 1)
                update(g, 1, hT[1])
                pe.wait_ge(s_ye, 2 * g + 2)
                transposed(bT[0], [yd[s][:, c, :] for c in range(C)]).then_inc(p_hd, 1)
                wait(pe, v_out, Q * g)
                output(bO[0], uT[0], False).then_inc(p_out, 1)
                pe.wait_ge(a_z, g + 1)
                mm(bM[:, :], V[:, :], zT[:, :], start=True, stop=True).then_inc(p_m, 1)
                pe.wait_ge(a_hd, g + 1)
                mm(bP[1][:, :], U1a[:, :], hdT[:, :], start=True, stop=True).then_inc(p_pree, 1)
                pe.wait_ge(a_u, Q * g + 2)
                update(g, 2, hT[0])
                pe.wait_ge(s_y3, g + 1)
                transposed(bT[1], quarter(s, 3)).then_inc(p_hT, 1)
                output(bO[1], uT[1], False).then_inc(p_out, 1)
                pe.wait_ge(v_out, Q * g + 1)
                bias(bO[0], g)
                pe.wait_ge(a_u, Q * g + 3)
                update(g, 3, hT[1])
                output(bO[0], uT[2], True).then_inc(p_out, 1)
                if more:
                    pe.wait_ge(s_y, (Q - 1) * g + 4)
                    transposed(bT[0], quarter(1 - s, 0)).then_inc(p_hT, 1)

                def update_edges():
                    wait(pe, v_oute, g)
                    pe.wait_ge(a_ue, g + 1)
                    output(bE, ueT, False).then_inc(p_oute, 1)

                if more:
                    update_edges()
                pe.wait_ge(v_out, Q * g + 2)
                bias(bO[1], g)
                pe.wait_ge(a_u, Q * g + 4)
                output(bO[1], uT[3], True).then_inc(p_out, 1)
                if not more:
                    update_edges()

            for k in range(R):
                group(0, k)
            with pe.Fori(1, LAST // R) as i:
                for k in range(R):
                    group(i, k)
            group(LAST // R, 0)


_INS = ['x', 'src', 'dst', 'edge_attr_64', 'L0_gnn_msg_w1', 'L0_gnn_msg_b1', 'L0_gnn_msg_w2', 'L0_gnn_msg_b2',
        'L0_gnn_upd_w1', 'L0_gnn_upd_b1', 'L0_gnn_upd_w2', 'L0_gnn_upd_b2']


def kernel(**inputs):
    import numpy as _np
    import concourse.bacc as _bacc
    from concourse import mybir as _mybir
    from concourse.bass_utils import run_bass_kernel_spmd as _run

    nc = _bacc.Bacc("TRN2", target_bir_lowering=False, num_devices=1)
    arrays, args = {}, []
    for name in _INS:
        a = _np.ascontiguousarray(inputs[name])
        arrays[f"in_{name}_dram"] = a
        args.append(nc.dram_tensor(f"in_{name}_dram", a.shape, _mybir.dt.from_np(a.dtype), kind="ExternalInput").ap())
    x = arrays["in_x_dram"]
    args.append(nc.dram_tensor("out_dram", x.shape, _mybir.dt.from_np(x.dtype), kind="ExternalOutput").ap())
    bass_preln_gnn(nc, *args)
    r = _run(nc, [arrays], core_ids=[0])
    return r.results[0]["out_dram"]
```
